# Optimizing a Trainium2 kernel written in Bass

```python
import numpy as np
import jax
import jax.numpy as jnp

def _softmax(x, axis=-1):
    return jax.nn.softmax(x, axis=axis)

def _gelu(x):
    return jax.nn.gelu(x, approximate=True)

def _silu(x):
    return jax.nn.silu(x)

def _sigmoid(x):
    return jax.nn.sigmoid(x)

def _layernorm(x, axis=-1, eps=1e-05):
    m = jnp.mean(x, axis=axis, keepdims=True)
    v = jnp.var(x, axis=axis, keepdims=True)
    return (x - m) / jnp.sqrt(v + eps)

def _scatter_add(tgt, idx, src, axis=0):
    return tgt.at[idx].add(src)

def _segment_sum(src, seg, n):
    return jax.ops.segment_sum(src, seg, n)
kernel_name = 'mk_xattn_seq_d1_seqx_r8_f6de38'

def setup_inputs(seed: int=0):
    np.random.seed(seed)
    _w = jnp.asarray

    def _rec_inputs():
        import jax
        import jax.numpy as jnp
        _rk = jax.random.key(seed)
        x = 7.22e-05 + 1 * jax.random.normal(jax.random.fold_in(_rk, 1), (32, 56, 512), jnp.float32)
        _lenS = 56 - jax.random.randint(jax.random.fold_in(_rk, 7), (32,), 0, max(1, 56 // 4) + 1, jnp.int32)
        _lenS2 = 1500 - jax.random.randint(jax.random.fold_in(_rk, 8), (32,), 0, max(1, 1500 // 4) + 1, jnp.int32)
        _ctx_4096P = jax.random.normal(jax.random.fold_in(_rk, 11), (32, 16, 512), jnp.float32)
        _ctx_4096c = jax.random.dirichlet(jax.random.fold_in(_rk, 511), 0.3 * jnp.ones((16,), jnp.float32), (32, 1500))
        _ctx_4096t = jnp.einsum('bsk,bkd->bsd', _ctx_4096c, _ctx_4096P)
        _ctx_4096t = _ctx_4096t * jax.lax.rsqrt(jnp.mean(jnp.square(_ctx_4096t)) + 1e-12) * 0.953939
        ctx_4096 = 4.13588e-05 + 0.999923 * (_ctx_4096t + 0.3 * jax.random.normal(jax.random.fold_in(_rk, 611), (32, 1500, 512), jnp.float32))
        _validS = jnp.arange(56)[None, :] < _lenS[:, None]
        _validS2 = jnp.arange(1500)[None, :] < _lenS2[:, None]
        _causal = jnp.tril(jnp.ones((56, 56), dtype=bool))
        mask_BxS2_ik0 = jnp.where(jnp.broadcast_to(_validS2[:, :], (32, 1500)), 0, 1).astype(jnp.int32)
        return (x, ctx_4096, mask_BxS2_ik0)
    x, ctx_4096, mask_BxS2_ik0 = _rec_inputs()

    def _L0_xattn_setup():
        import jax, jax.numpy as jnp
        import numpy as np
        H = 512
        NH = 32
        HD = H // NH
        key = jax.random.key(seed)
        ks = jax.random.split(key, 12)
        B, L, V = (2, 128, 128)
        s = 1.0 / np.sqrt(H)
        return {'hidden_states': jax.random.normal(ks[0], (B, L, H), jnp.float32), 'vision_features': jax.random.normal(ks[1], (B, V, H), jnp.float32), 'attention_mask': jax.random.randint(ks[2], (B, V), 0, 2, jnp.int32), 'Wq': jax.random.normal(ks[3], (H, H), jnp.float32) * s, 'bq': jnp.zeros((H,), jnp.float32), 'Wk': jax.random.normal(ks[4], (H, H), jnp.float32) * s, 'bk': jnp.zeros((H,), jnp.float32), 'Wv': jax.random.normal(ks[5], (H, H), jnp.float32) * s, 'bv': jnp.zeros((H,), jnp.float32), 'Wo': jax.random.normal(ks[6], (H, H), jnp.float32) * s, 'bo': jnp.zeros((H,), jnp.float32), 'ln_g': jnp.ones((H,), jnp.float32), 'ln_b': jnp.zeros((H,), jnp.float32)}
    _L0_xattn_all = _L0_xattn_setup()
    _L0_xattn_in = {k: v for k, v in _L0_xattn_all.items() if k in ('Wq', 'bq', 'Wk', 'bk', 'Wv', 'bv', 'Wo', 'bo', 'ln_g', 'ln_b')}
    del _L0_xattn_all
    return {'x': x, 'ctx_4096': ctx_4096, 'mask_BxS2_ik0': mask_BxS2_ik0, 'L0_xattn_Wq': _L0_xattn_in['Wq'], 'L0_xattn_bq': _L0_xattn_in['bq'], 'L0_xattn_Wk': _L0_xattn_in['Wk'], 'L0_xattn_bk': _L0_xattn_in['bk'], 'L0_xattn_Wv': _L0_xattn_in['Wv'], 'L0_xattn_bv': _L0_xattn_in['bv'], 'L0_xattn_Wo': _L0_xattn_in['Wo'], 'L0_xattn_bo': _L0_xattn_in['bo'], 'L0_xattn_ln_g': _L0_xattn_in['ln_g'], 'L0_xattn_ln_b': _L0_xattn_in['ln_b']}

def reference(x, ctx_4096, mask_BxS2_ik0, L0_xattn_Wq, L0_xattn_bq, L0_xattn_Wk, L0_xattn_bk, L0_xattn_Wv, L0_xattn_bv, L0_xattn_Wo, L0_xattn_bo, L0_xattn_ln_g, L0_xattn_ln_b):
    import jax
    import jax.numpy as jnp

    def _L0_xattn_ref(hidden_states, vision_features, attention_mask, Wq, bq, Wk, bk, Wv, bv, Wo, bo, ln_g, ln_b):
        import jax, jax.numpy as jnp
        import numpy as np
        H = 512
        NH = 32
        HD = H // NH
        B, L, _ = hidden_states.shape
        Vn = vision_features.shape[1]
        Q = (hidden_states @ Wq.T + bq).reshape(B, L, NH, HD)
        K = (vision_features @ Wk.T + bk).reshape(B, Vn, NH, HD)
        Vv = (vision_features @ Wv.T + bv).reshape(B, Vn, NH, HD)
        scores = jnp.einsum('blhd,bvhd->bhlv', Q, K) / np.sqrt(HD).astype(np.float32)
        mask = (attention_mask != 0)[:, None, None, :]
        scores = jnp.where(mask, scores, -jnp.inf)
        attn = jax.nn.softmax(scores, axis=-1)
        ctx = jnp.einsum('bhlv,bvhd->blhd', attn, Vv).reshape(B, L, H)
        attn_out = ctx @ Wo.T + bo
        x = hidden_states + attn_out
        mu = jnp.mean(x, axis=-1, keepdims=True)
        var = jnp.mean(jnp.square(x - mu), axis=-1, keepdims=True)
        return (x - mu) / jnp.sqrt(var + 1e-05) * ln_g + ln_b
    x = _L0_xattn_ref(x, ctx_4096, mask_BxS2_ik0, L0_xattn_Wq, L0_xattn_bq, L0_xattn_Wk, L0_xattn_bk, L0_xattn_Wv, L0_xattn_bv, L0_xattn_Wo, L0_xattn_bo, L0_xattn_ln_g, L0_xattn_ln_b)
    return x

_drawn_inputs = setup_inputs


def setup_inputs(seed=0):
    import zlib

    import numpy as np

    out = dict(_drawn_inputs(seed))
    spreads = {'L0_xattn_bq': (0.0, 0.397),
     'L0_xattn_bk': (0.0, 0.8),
     'L0_xattn_bv': (0.0, 0.1),
     'L0_xattn_bo': (0.0, 0.1),
     'L0_xattn_ln_g': (1.0, 0.2),
     'L0_xattn_ln_b': (0.0, 0.1)}
    factors = {}
    for name, (base, spread) in spreads.items():
        noise = np.random.default_rng([zlib.crc32(name.encode()), seed]).standard_normal(out[name].shape)
        drawn = base * np.exp(spread * noise) if base else spread * noise
        out[name] = jnp.asarray(drawn.astype(out[name].dtype))
    for name, factor in factors.items():
        out[name] = (out[name] * factor).astype(out[name].dtype)
    return out
```

```python
from contextlib import ExitStack

import concourse.bass as bass
from concourse import mybir

F32 = mybir.dt.float32
F32R = mybir.dt.float32r
I32 = mybir.dt.int32
ALU = mybir.AluOpType
ACT = mybir.ActivationFunctionType
AX = mybir.AxisListType

P = 128
B, L, S, D = 32, 56, 1500, 512
NH, HD = 32, 16
KT = D // P
NG = 4
HG = NH // NG
SC = 125
NC_ = S // SC
NP = 6
SP_ = S // NP
NQ = 3
SQ = S // NQ
CQ = NC_ // NQ
NR = 3
HW = HG * L
HALF = HW // 2
VW = HD + 1
NQB = 4
BPB = B // NQB
ROWS = B * L
NT = ROWS // P
EPS = 1e-5
MASKED = -3.0e38
FLOOR = -1.0e38
MQ = HW // 4


def build_attention(nc, ctxT, maskT, xT, x_rows, wqT, wkT, wvT, woT, bq, bk, bv_col, bo, ln_g,
                    ln_b, ident_in, head_mask_in, den_sel_in, q_scratch, att_scratch, out):
    with ExitStack() as ctx:
        def sb(name, shape, dt=F32):
            return ctx.enter_context(nc.sbuf_tensor(name + "_sb", shape, dt))

        def psum(name, shape):
            return ctx.enter_context(nc.psum_tensor(name, shape, F32))

        def sem(name):
            return ctx.enter_context(nc.semaphore(name))

        s_buf = sb("s_buf", [P, 2, NC_, HW])
        wk_hi = sb("wk_hi", [P, KT, D], F32R)
        wk_lo = sb("wk_lo", [P, KT, D], F32R)
        wv_hi = sb("wv_hi", [P, KT, D], F32R)
        wv_lo = sb("wv_lo", [P, KT, D], F32R)
        c_hi = sb("c_hi", [P, KT, S], F32R)
        c_lo = sb("c_lo", [P, KT, S], F32R)
        raw = sb("raw", [P, NR, KT, SP_])
        k_a = sb("k_a", [P, S], F32R)
        k_b = sb("k_b", [P, S], F32R)
        v_sb = sb("v_sb", [P, NC_, NH, VW])
        qd_hi = sb("qd_hi", [P, 2, 2, HALF], F32R)
        qd_lo = sb("qd_lo", [P, 2, 2, HALF], F32R)
        q_raw = sb("q_raw", [P, NG, 2, L])
        q_hi = sb("q_hi", [P, NG, 2, L], F32R)
        q_lo = sb("q_lo", [P, NG, 2, L])
        mx = sb("mx", [P, 2, HW])
        mx_one = sb("mx_one", [P, HW])
        col_max = sb("col_max", [MQ, 4])
        diag = sb("diag", [MQ, 4, MQ])
        mask_i = sb("mask_i", [P, NC_], I32)
        mask_bias = sb("mask_bias", [P, NC_])
        o_raw = sb("o_raw", [P, 2 * L])
        o_rec = sb("o_rec", [P, 2 * L])
        o_mul = sb("o_mul", [P, 2 * L])
        o_out = sb("o_out", [P, NG, 2, L])
        ident = sb("ident", [P, P])
        ones = sb("ones", [P, P])
        head_mask = sb("head_mask", [P, 4])
        den_sel = sb("den_sel", [P, P])
        bq_sb = sb("bq_sb", [P, KT])
        bq_scaled = sb("bq_scaled", [P, KT])
        bk_sb = sb("bk_sb", [P, KT])
        bv_sb = sb("bv_sb", [P, NG, 2])

        stage = s_buf[:, :, :, :].rearrange("p a c n -> p (a c n)")
        wk_raw = stage[:, 0:KT * D]
        wv_raw = stage[:, KT * D:2 * KT * D]
        wq_raw = stage[:, 2 * KT * D:3 * KT * D].rearrange("p (k n) -> p k n", k=KT)
        NX = BPB * L
        x_at = 3 * KT * D
        x_raw = stage[:, x_at:x_at + 2 * KT * NX].rearrange("p (s k n) -> p s k n", s=2, k=KT)
        q_stage = v_sb[:, :, :, :].rearrange("p c h w -> p (c h w)")[:, 0:4 * NX].rearrange(
            "p (s n) -> p s n", s=4)

        ps_proj = [psum(f"ps_proj{i}", [P, 512]) for i in range(2)]
        ps_score = [psum(f"ps_score{i}", [P, 512]) for i in range(4)]
        ps_o = psum("ps_o", [P, 512])
        ps_max = psum("ps_max", [P, 512])

        weights_loaded = sem("weights_loaded")
        wq_loaded = sem("wq_loaded")
        consts_loaded = sem("consts_loaded")
        x_loaded = [sem(f"x_loaded{i}") for i in range(2)]
        weights_split_hi = sem("weights_split_hi")
        weights_split_lo = sem("weights_split_lo")
        memsets_done = sem("memsets_done")
        bq_ready = sem("bq_ready")
        qproj_done = sem("qproj_done")
        q_evicted = sem("q_evicted")
        q_stored = [sem(f"q_stored{i}") for i in range(4)]
        raw_loaded = [sem(f"raw_loaded{i}") for i in range(NR)]
        batch_loaded = sem("batch_loaded")
        c_hi_ready = sem("c_hi_ready")
        c_lo_ready = sem("c_lo_ready")
        q_hi_ready = sem("q_hi_ready")
        q_lo_ready = sem("q_lo_ready")
        qd_ready = sem("qd_ready")
        mask_ready = sem("mask_ready")
        kproj_done = sem("kproj_done")
        k_hi_ready = sem("k_hi_ready")
        k_lo_ready = sem("k_lo_ready")
        vproj_done = sem("vproj_done")
        v_ready = sem("v_ready")
        scores_done = sem("scores_done")
        s_ready = sem("s_ready")
        max_step = sem("max_step")
        maxT_done = sem("maxT_done")
        colmax_ready = sem("colmax_ready")
        diag_ready = sem("diag_ready")
        spread_done = sem("spread_done")
        shifted = sem("shifted")
        exp_done = sem("exp_done")
        pv_done = sem("pv_done")
        o_raw_ready = sem("o_raw_ready")
        den_done = sem("den_done")
        rec_ready = sem("rec_ready")
        mul_ready = sem("mul_ready")
        o_ready = sem("o_ready")
        att_stored = sem("att_stored")

        NMAX = 6
        SH = 4
        NSH = NC_ // SH
        QDMA = 32
        BATCH_DMA = QDMA + 16

        block = ctx.enter_context(nc.Block())

        @block.sync
        def _(sp):
            sp.dma_start(wq_raw, wqT.rearrange("p (k n) -> p k n", k=KT)).then_inc(wq_loaded, 16)
            sp.dma_start(x_raw[:, 0], xT[0]).then_inc(x_loaded[0], 16)
            for dst, src in ((ident[:, :], ident_in), (head_mask[:, :], head_mask_in),
                             (den_sel[:, :], den_sel_in), (bq_sb[:, :], bq), (bk_sb[:, :], bk),
                             (bv_sb[:, :, :], bv_col.rearrange("p (g s) -> p g s", g=NG))):
                sp.dma_start(dst, src).then_inc(consts_loaded, 16)
            sp.dma_start(x_raw[:, 1], xT[1]).then_inc(x_loaded[1], 16)
            sp.dma_start(wk_raw, wkT).then_inc(weights_loaded, 16)
            sp.dma_start(wv_raw, wvT).then_inc(weights_loaded, 16)

            def load_piece(b, i, first):
                if not (first and i < NR):
                    sp.wait_ge(c_hi_ready, b * NP + (i + 1 - NR))
                    sp.wait_ge(c_lo_ready, b * NP + (i + 1 - NR))
                sp.dma_start(raw[:, i % NR], ctxT[bass.ds(b, 1), i].rearrange(
                    "o p k n -> (o p) k n")).then_inc(raw_loaded[i % NR], 16)

            def load_queries(b, first):
                if not first:
                    sp.wait_ge(q_lo_ready, b)
                    sp.wait_ge(mask_ready, b)
                for half in range(2):
                    sp.dma_start(q_raw[64 * half:64 * half + 64], q_scratch[bass.ds(b, 1)].rearrange(
                        "o p g s l -> (o p) g s l")).then_inc(batch_loaded, 16)
                sp.dma_start(mask_i[0:SC, :], maskT[bass.ds(b, 1)].rearrange(
                    "o p c -> (o p) c")).then_inc(batch_loaded, 16)

            def store_attention(b):
                sp.wait_ge(o_ready, (b + 1) * NG)
                for j in range(4):
                    sp.dma_start(
                        att_scratch[:, j, :, bass.ds(b, 1)].rearrange("s d o l -> d s (o l)"),
                        o_out[32 * j:32 * j + HD].rearrange("p g s l -> p (g s) l"),
                    ).then_inc(att_stored, 16)

            for i in range(NR):
                load_piece(0, i, True)
            for n in range(NQB):
                for g in range(NG):
                    i = n * NG + g
                    sp.wait_ge(q_evicted, i + 1)
                    for s in range(2):
                        sp.dma_start(
                            q_scratch[n * BPB:(n + 1) * BPB, :, g, s].rearrange("b p l -> p b l"),
                            q_stage[64 * s:64 * s + 64, i % 4].rearrange("p (b l) -> p b l", b=BPB),
                        ).then_inc(q_stored[i % 4], 16)
                if n + 2 < NQB:
                    sp.wait_ge(qproj_done, (n + 1) * NG)
                    sp.dma_start(x_raw[:, n % 2], xT[n + 2]).then_inc(x_loaded[n % 2], 16)
            for i in range(4):
                sp.wait_ge(q_stored[i], 32 * NQB)
            load_queries(0, True)
            for i in range(NR, NP):
                load_piece(0, i, True)
            for i in range(NP):
                if i == NR:
                    load_queries(1, False)
                load_piece(1, i, False)
            with sp.Fori(1, B - 1) as b:
                store_attention(b - 1)
                for i in range(NP):
                    if i == NR:
                        load_queries(b + 1, False)
                    load_piece(b + 1, i, False)
            store_attention(B - 2)
            store_attention(B - 1)
            sp.wait_ge(att_stored, 64 * B)

        @block.tensor
        def _(pe):
            pe.wait_ge(wq_loaded, 16)
            for n in range(NQB):
                pe.wait_ge(x_loaded[n % 2], 16 * (n // 2 + 1))
                for g in range(NG):
                    i = n * NG + g
                    if i >= 4:
                        pe.wait_ge(q_evicted, i - 3)
                    for k in range(KT):
                        mm = nc.tensor.matmul(ps_score[i % 4][:, 0:NX], wq_raw[:, k, g * P:(g + 1) * P],
                                              x_raw[:, n % 2, k], start=(k == 0), stop=(k == KT - 1))
                    mm.then_inc(qproj_done, 1)
            pe.wait_ge(consts_loaded, 96)
            pe.wait_ge(memsets_done, 3)
            pe.wait_ge(weights_split_hi, 2)
            pe.wait_ge(weights_split_lo, 2)

            def project_k(t, b, g, q, first):
                if g == 0:
                    pe.wait_ge(c_hi_ready, b * NP + 2 * q + 2)
                    pe.wait_ge(c_lo_ready, b * NP + 2 * q + 2)
                if g == 2 and q < 2:
                    pe.wait_ge(v_ready, b * NC_ + NC_ - 1 + q)
                elif not (first and g == 0 and q < 2):
                    pe.wait_ge(k_lo_ready, t * NQ + q - 1)
                bank = ps_proj[(g + q) % 2][:, 0:SQ]
                keys = slice(q * SQ, (q + 1) * SQ)
                cols = slice(g * P, (g + 1) * P)
                for k in range(KT):
                    nc.tensor.matmul(bank, wk_hi[:, k, cols], c_hi[:, k, keys], start=(k == 0), stop=False)
                    nc.tensor.matmul(bank, wk_hi[:, k, cols], c_lo[:, k, keys], start=False, stop=False)
                    mm = nc.tensor.matmul(bank, wk_lo[:, k, cols], c_hi[:, k, keys], start=False,
                                          stop=(k == KT - 1))
                mm.then_inc(kproj_done, 1)

            def project_v(b, t):
                for c in range(NC_):
                    keys = slice(c * SC, (c + 1) * SC)
                    if c < 2:
                        pe.wait_ge(k_lo_ready, t * NQ + 2 + c)
                    else:
                        pe.wait_ge(v_ready, b * NC_ + c - 1)
                    bank = ps_proj[c % 2][0:SC, :]
                    for k in range(KT):
                        hi, lo = c_hi[:, k, keys], c_lo[:, k, keys]
                        nc.tensor.matmul(bank, hi, wv_hi[:, k], start=(k == 0), stop=False)
                        nc.tensor.matmul(bank, hi, wv_lo[:, k], start=False, stop=False)
                        mm = nc.tensor.matmul(bank, lo, wv_hi[:, k], start=False, stop=(k == KT - 1))
                    mm.then_inc(vproj_done, 1)

            def scores(t, g, first):
                pe.wait_ge(qd_ready, t + 1)
                for c in range(NC_):
                    if c % CQ == 0:
                        pe.wait_ge(k_hi_ready, t * NQ + c // CQ + 1)
                        pe.wait_ge(k_lo_ready, t * NQ + c // CQ + 1)
                    if not (first and g == 0 and c < 4):
                        pe.wait_ge(s_ready, t * NC_ + c - 3)
                    bank = ps_score[c % 4]
                    for s, kk in enumerate((k_a, k_b)):
                        w = kk[:, c * SC:(c + 1) * SC]
                        o = bank[0:SC, s * HALF:(s + 1) * HALF]
                        nc.tensor.matmul(o, w, qd_hi[:, g % 2, s], start=True, stop=False)
                        mm = nc.tensor.matmul(o, w, qd_lo[:, g % 2, s], start=False, stop=True)
                    mm.then_inc(scores_done, 1)

            def max_transposes(t):
                pe.wait_ge(max_step, (t + 1) * NMAX)
                if not (isinstance(t, int) and t == 0):
                    pe.wait_ge(shifted, t * NSH)
                for i in range(4):
                    mm = nc.tensor.transpose(ps_max[0:MQ, i * SC:(i + 1) * SC],
                                             mx_one[0:SC, i * MQ:(i + 1) * MQ], ident[0:SC, 0:SC])
                mm.then_inc(maxT_done, 1)

            def max_spread(t):
                pe.wait_ge(diag_ready, t + 1)
                nc.tensor.matmul(ps_max[0:SC, 0:HW], ones[0:MQ, 0:SC],
                                 diag[:, :, :].rearrange("p a n -> p (a n)"),
                                 start=True, stop=True).then_inc(spread_done, 1)

            def times_v(t, g):
                if not (isinstance(t, int) and t == 0):
                    pe.wait_ge(o_raw_ready, t)
                    pe.wait_ge(rec_ready, t)
                for c in range(NC_):
                    if c % SH == 0:
                        pe.wait_ge(exp_done, t * NSH + c // SH + 1)
                    for s in range(2):
                        for j in range(4):
                            hh = 4 * s + j
                            mm = nc.tensor.matmul(
                                ps_o[32 * j:32 * j + VW, s * L:(s + 1) * L],
                                v_sb[0:SC, c, g * HG + hh], s_buf[0:SC, g % 2, c, hh * L:(hh + 1) * L],
                                start=(c == 0 and s == 0), stop=(c == NC_ - 1 and s == 1),
                                skip_group_check=True)
                mm.then_inc(pv_done, 1)

            def denominators(t):
                pe.wait_ge(o_raw_ready, t + 1)
                nc.tensor.matmul(ps_o[:, 2 * L:4 * L], den_sel[:, :], o_raw[:, :], start=True,
                                 stop=True, skip_group_check=True).then_inc(den_done, 1)

            def step(b, g, first):
                t = b * NG + g
                begun = not (first and g == 0)
                ended = not (first and g < 2)
                project_k(t, b, g, 0, first)
                if begun:
                    max_transposes(t - 1)
                project_k(t, b, g, 1, first)
                if begun:
                    max_spread(t - 1)
                project_k(t, b, g, 2, first)
                if ended:
                    times_v(t - 2, (g - 2) % NG)
                if g == 1:
                    project_v(b, t)
                scores(t, g, first)
                if ended:
                    denominators(t - 2)

            for g in range(NG):
                step(0, g, True)
            with pe.Fori(1, B) as b:
                for g in range(NG):
                    step(b, g, False)
            last = B * NG - 1
            pe.wait_ge(v_ready, B * NC_)
            times_v(last - 1, NG - 2)
            max_transposes(last)
            max_spread(last)
            denominators(last - 1)
            times_v(last, NG - 1)
            denominators(last)

        @block.scalar
        def _(act):
            act.wait_ge(consts_loaded, 96)
            nc.scalar.mul(bq_scaled[:, :], bq_sb[:, :], HD ** -0.5).then_inc(bq_ready, 1)
            act.wait_ge(bq_ready, 1)
            for i in range(NQB * NG):
                act.wait_ge(qproj_done, i + 1)
                if i >= 4:
                    act.wait_ge(q_stored[i % 4], 32 * (i // 4))
                nc.scalar.activation(q_stage[:, i % 4], ps_score[i % 4][:, 0:NX], ACT.Identity,
                                     bias=bq_scaled[:, i % NG:i % NG + 1],
                                     scale=HD ** -0.5).then_inc(q_evicted, 1)
            act.wait_ge(weights_loaded, 32)
            nc.scalar.copy(wk_hi[:, :, :].rearrange("p k n -> p (k n)"), wk_raw).then_inc(weights_split_hi, 1)
            nc.scalar.copy(wv_hi[:, :, :].rearrange("p k n -> p (k n)"), wv_raw).then_inc(weights_split_hi, 1)

            def split_hi(b, i, first):
                act.wait_ge(raw_loaded[i % NR], (b * 2 + i // NR + 1) * 16)
                if not first:
                    act.wait_ge(kproj_done, (b * NG - 1) * NQ + i // 2 + 1)
                nc.scalar.copy(c_hi[:, :, i * SP_:(i + 1) * SP_], raw[:, i % NR]).then_inc(c_hi_ready, 1)

            def round_queries(b):
                act.wait_ge(batch_loaded, (b + 1) * BATCH_DMA)
                if not (isinstance(b, int) and b == 0):
                    act.wait_ge(qd_ready, b * NG)
                nc.scalar.copy(q_hi[:, :, :, :], q_raw[:, :, :, :]).then_inc(q_hi_ready, 1)

            def evict_k_hi(t, g, q, first):
                act.wait_ge(kproj_done, t * NQ + q + 1)
                if not (first and g == 0) and q == 0:
                    act.wait_ge(scores_done, t * NC_)
                cols = slice(q * SQ, (q + 1) * SQ)
                bank = ps_proj[(g + q) % 2]
                nc.scalar.activation(k_a[0:64, cols], bank[0:64, 0:SQ], ACT.Identity,
                                     bias=bk_sb[0:64, g:g + 1])
                nc.scalar.activation(k_b[64:128, cols], bank[64:128, 0:SQ], ACT.Identity,
                                     bias=bk_sb[64:128, g:g + 1]).then_inc(k_hi_ready, 1)

            def exps(t, g):
                for i in range(NSH):
                    act.wait_ge(shifted, t * NSH + i + 1)
                    part = s_buf[0:SC, g % 2, i * SH:(i + 1) * SH]
                    nc.scalar.activation(part, part, ACT.Exp).then_inc(exp_done, 1)

            def evict_v(b, first):
                if not first:
                    act.wait_ge(pv_done, b * NG)
                for c in range(NC_):
                    act.wait_ge(vproj_done, b * NC_ + c + 1)
                    nc.scalar.copy(v_sb[0:SC, c, :, 0:HD], ps_proj[c % 2][0:SC, :].rearrange(
                        "p (h d) -> p h d", h=NH)).then_inc(v_ready, 1)

            def evict_scores(t, b, g, first):
                if g == 0:
                    act.wait_ge(mask_ready, b + 1)
                if not (first and g < 2):
                    act.wait_ge(pv_done, t - 1)
                for c in range(NC_):
                    act.wait_ge(scores_done, t * NC_ + c + 1)
                    nc.scalar.activation(s_buf[0:SC, g % 2, c], ps_score[c % 4][0:SC, 0:HW],
                                         ACT.Identity, bias=mask_bias[0:SC, c:c + 1]).then_inc(s_ready, 1)

            for i in range(NP):
                split_hi(0, i, True)
            round_queries(0)

            def step(b, g, first, last):
                t = b * NG + g
                for q in range(NQ):
                    evict_k_hi(t, g, q, first)
                if not (first and g == 0):
                    exps(t - 1, (g - 1) % NG)
                if g == 1:
                    evict_v(b, first)
                if g == 3 and not last:
                    round_queries(b + 1)
                if g == 3 and not last:
                    for i in range(NP):
                        split_hi(b + 1, i, False)
                evict_scores(t, b, g, first)

            act.wait_ge(weights_split_lo, 2)
            act.wait_ge(memsets_done, 3)
            for g in range(NG):
                step(0, g, True, False)
            with act.Fori(1, B - 1) as b:
                for g in range(NG):
                    step(b, g, False, False)
            for g in range(NG):
                step(B - 1, g, False, True)
            exps(B * NG - 1, NG - 1)

        @block.vector
        def _(dve):
            nc.vector.memset(ps_o[:, :], 0.0).then_inc(memsets_done, 1)
            nc.vector.memset(ones[:, :], 1.0).then_inc(memsets_done, 1)
            for hi, lo, w, n in ((wk_hi, wk_lo, wk_raw, 1), (wv_hi, wv_lo, wv_raw, 2)):
                dve.wait_ge(weights_split_hi, n)
                nc.vector.tensor_tensor(lo[:, :, :].rearrange("p k n -> p (k n)"), w,
                                        hi[:, :, :].rearrange("p k n -> p (k n)").bitcast(F32),
                                        ALU.subtract).then_inc(weights_split_lo, 1)
            for i in range(4):
                dve.wait_ge(q_stored[i], 32 * NQB)
            nc.vector.memset(v_sb[:, :, :, HD:VW], 1.0).then_inc(memsets_done, 1)

            def evict_k_lo(t, g, q):
                dve.wait_ge(k_hi_ready, t * NQ + q + 1)
                cols = slice(q * SQ, (q + 1) * SQ)
                bank = ps_proj[(g + q) % 2]
                nc.vector.scalar_tensor_tensor(
                    out=k_a[64:128, cols], in0=bank[0:64, 0:SQ], scalar=bk_sb[0:64, g:g + 1],
                    in1=k_a[0:64, cols].bitcast(F32), op0=ALU.add, op1=ALU.subtract)
                nc.vector.scalar_tensor_tensor(
                    out=k_b[0:64, cols], in0=bank[64:128, 0:SQ], scalar=bk_sb[64:128, g:g + 1],
                    in1=k_b[64:128, cols].bitcast(F32), op0=ALU.add, op1=ALU.subtract).then_inc(k_lo_ready, 1)

            def chunk_max(t, g, first):
                part = s_buf[0:SC, g % 2]
                acc = mx[0:SC]
                if not (first and g == 0):
                    dve.wait_ge(maxT_done, t)
                for i in range(5):
                    dve.wait_ge(s_ready, t * NC_ + 2 * i + 4)
                    if i:
                        dve.wait_ge(max_step, t * NMAX + i)
                    nc.vector.tensor_tensor(acc, part[:, 2 * i + 2:2 * i + 4], acc if i else part[:, 0:2],
                                            ALU.max).then_inc(max_step, 1)
                dve.wait_ge(max_step, t * NMAX + 5)
                nc.vector.scalar_tensor_tensor(out=mx_one[0:SC], in0=acc[:, 0], scalar=FLOOR, in1=acc[:, 1],
                                               op0=ALU.max, op1=ALU.max).then_inc(max_step, 1)

            def mask_to_bias(b):
                dve.wait_ge(batch_loaded, (b + 1) * BATCH_DMA)
                if not (isinstance(b, int) and b == 0):
                    dve.wait_ge(s_ready, b * NG * NC_)
                nc.vector.tensor_scalar(mask_bias[0:SC, :], mask_i[0:SC, :], 0, MASKED, ALU.is_equal,
                                        ALU.mult).then_inc(mask_ready, 1)

            def partition_max(t):
                dve.wait_ge(maxT_done, t + 1)
                nc.vector.tensor_reduce(col_max[:, :], ps_max[0:MQ, 0:4 * SC].rearrange(
                    "p (a n) -> p a n", a=4), AX.X, ALU.max).then_inc(colmax_ready, 1)
                dve.wait_ge(colmax_ready, t + 1)
                nc.vector.tensor_tensor(
                    diag[:, :, :], ident[0:MQ, 0:MQ].unsqueeze(1).to_broadcast([MQ, 4, MQ]),
                    col_max[:, :].unsqueeze(2).to_broadcast([MQ, 4, MQ]), ALU.mult).then_inc(diag_ready, 1)

            def shift(t, g):
                dve.wait_ge(spread_done, t + 1)
                top = ps_max[0:SC, 0:HW].unsqueeze(1).to_broadcast([SC, SH, HW])
                for i in range(NSH):
                    part = s_buf[0:SC, g % 2, i * SH:(i + 1) * SH]
                    nc.vector.tensor_tensor(part, part, top, ALU.subtract).then_inc(shifted, 1)

            def take_output(t):
                dve.wait_ge(pv_done, t + 1)
                if not (isinstance(t, int) and t == 0):
                    dve.wait_ge(mul_ready, t)
                nc.vector.tensor_copy(o_raw[:, :], ps_o[:, 0:2 * L]).then_inc(o_raw_ready, 1)

            def normalise(t, g, b):
                dve.wait_ge(den_done, t + 1)
                nc.vector.reciprocal(o_rec[:, :], ps_o[:, 2 * L:4 * L]).then_inc(rec_ready, 1)
                dve.wait_ge(rec_ready, t + 1)
                nc.vector.tensor_tensor(o_mul[:, :], o_raw[:, :], o_rec[:, :], ALU.mult).then_inc(mul_ready, 1)
                dve.wait_ge(mul_ready, t + 1)
                if g == 0 and not (isinstance(b, int) and b == 0):
                    dve.wait_ge(att_stored, b * 64)
                nc.vector.tensor_tensor(
                    o_out[:, g], o_mul[:, :].rearrange("p (s l) -> p s l", s=2),
                    bv_sb[:, g].unsqueeze(2).to_broadcast([P, 2, L]), ALU.add).then_inc(o_ready, 1)

            def step(b, g, first, last):
                t = b * NG + g
                begun = not (first and g == 0)
                ended = not (first and g < 2)
                evict_k_lo(t, g, 0)
                if begun:
                    partition_max(t - 1)
                evict_k_lo(t, g, 1)
                evict_k_lo(t, g, 2)
                if begun:
                    shift(t - 1, (g - 1) % NG)
                if ended:
                    take_output(t - 2)
                chunk_max(t, g, first)
                if g == 3 and not last:
                    mask_to_bias(b + 1)
                if ended:
                    normalise(t - 2, (g - 2) % NG, b if g >= 2 else b - 1)

            mask_to_bias(0)
            for g in range(NG):
                step(0, g, True, False)
            with dve.Fori(1, B - 1) as b:
                for g in range(NG):
                    step(b, g, False, False)
            for g in range(NG):
                step(B - 1, g, False, True)
            last = B * NG - 1
            take_output(last - 1)
            partition_max(last)
            shift(last, NG - 1)
            normalise(last - 1, NG - 2, B - 1)
            take_output(last)
            normalise(last, NG - 1, B - 1)

        @block.gpsimd
        def _(pool):
            def split_lo(b, i):
                pool.wait_ge(c_hi_ready, b * NP + i + 1)
                keys = slice(i * SP_, (i + 1) * SP_)
                nc.gpsimd.tensor_tensor(c_lo[:, :, keys], raw[:, i % NR], c_hi[:, :, keys].bitcast(F32),
                                        ALU.subtract).then_inc(c_lo_ready, 1)

            def split_queries(b):
                pool.wait_ge(q_hi_ready, b + 1)
                nc.gpsimd.tensor_tensor(q_lo[:, :, :, :], q_raw[:, :, :, :], q_hi[:, :, :, :].bitcast(F32),
                                        ALU.subtract).then_inc(q_lo_ready, 1)

            def query_blocks(t, b, g, first):
                if not (first and g < 2):
                    pool.wait_ge(scores_done, (t - 1) * NC_)
                pool.wait_ge(q_lo_ready, b + 1)
                for dst, src in ((qd_hi, q_hi), (qd_lo, q_lo)):
                    for s in range(2):
                        q = src[:, g, s] if src is q_lo else src[:, g, s].bitcast(F32)
                        last = nc.gpsimd.tensor_tensor(
                            dst[:, g % 2, s].rearrange("p (h l) -> p h l", h=4),
                            q.unsqueeze(1).to_broadcast([P, 4, L]),
                            head_mask[:, :].unsqueeze(2).to_broadcast([P, 4, L]), ALU.mult)
                last.then_inc(qd_ready, 1)

            pool.wait_ge(consts_loaded, 96)
            for i in range(NP):
                split_lo(0, i)
            split_queries(0)
            query_blocks(0, 0, 0, True)

            def step(b, g, first, last):
                t = b * NG + g
                if g < 3:
                    query_blocks(t + 1, b, g + 1, first)
                elif not last:
                    split_queries(b + 1)
                    query_blocks(t + 1, b + 1, 0, False)
                    for i in range(NP):
                        pool.wait_ge(kproj_done, t * NQ + i // 2 + 1)
                        split_lo(b + 1, i)

            for g in range(NG):
                step(0, g, True, False)
            with pool.Fori(1, B - 1) as b:
                for g in range(NG):
                    step(b, g, False, False)
            for g in range(NG):
                step(B - 1, g, False, True)


def build_output(nc, x_rows, woT, bo, ln_g, ln_b, att_scratch, out):
    with ExitStack() as ctx:
        def sb(name, shape):
            return ctx.enter_context(nc.sbuf_tensor(name + "_sb", shape, F32))

        def sem(name):
            return ctx.enter_context(nc.semaphore(name))

        wo_sb = sb("wo_sb", [P, KT, D])
        bo_sb = sb("bo_sb", [P, D])
        g_sb = sb("g_sb", [P, D])
        b_sb = sb("b_sb", [P, D])
        eps = sb("eps", [P, 1])
        att = sb("att", [P, 2, KT, P])
        xr = sb("xr", [P, 2, D])
        xb = sb("xb", [P, 2, D])
        y = sb("y", [P, 2, D])
        yn = sb("yn", [P, 2, D])
        yg = sb("yg", [P, 2, D])
        yo = sb("yo", [P, 2, D])
        stats = sb("stats", [P, 2, 6])
        mv = sb("mv", [P, 2, 2])
        std = sb("std", [P, 2, 1])
        rstd = sb("rstd", [P, 2, 1])
        nmean = sb("nmean", [P, 2, 1])
        ps = [ctx.enter_context(nc.psum_tensor(f"ps_out{i}", [P, 512], F32)) for i in range(2)]

        params_loaded = sem("params_loaded")
        att_loaded = [sem(f"att_loaded{i}") for i in range(2)]
        x_in = [sem(f"x_in{i}") for i in range(2)]
        eps_set = sem("eps_set")
        xb_ready = sem("xb_ready")
        out_done = sem("out_done")
        y_ready = sem("y_ready")
        stats_ready = sem("stats_ready")
        mv_ready = sem("mv_ready")
        std_ready = sem("std_ready")
        rstd_ready = sem("rstd_ready")
        nmean_ready = sem("nmean_ready")
        yn_ready = sem("yn_ready")
        yg_ready = sem("yg_ready")
        yo_ready = sem("yo_ready")
        out_stored = [sem(f"out_stored{i}") for i in range(2)]

        block = ctx.enter_context(nc.Block())
        attT = att_scratch.rearrange("(k s) j d b l -> k (s j d) (b l)", k=KT)

        @block.sync
        def _(sp):
            for dst, src in ((wo_sb[:, :, :], woT.rearrange("p (k n) -> p k n", k=KT)),
                             (bo_sb[:, :], bo.partition_broadcast(P)),
                             (g_sb[:, :], ln_g.partition_broadcast(P)),
                             (b_sb[:, :], ln_b.partition_broadcast(P))):
                sp.dma_start(dst, src).then_inc(params_loaded, 16)

            def load(i, s, first):
                if not first:
                    sp.wait_ge(out_done, 2 * i + s - 1)
                    sp.wait_ge(xb_ready, 2 * i + s - 1)
                sp.dma_start(att[:, s], attT[:, :, bass.ds(i * (2 * P) + s * P, P)].rearrange(
                    "k p n -> p k n")).then_inc(att_loaded[s], 16)
                sp.dma_start(xr[:, s], x_rows[bass.ds(i * (2 * P) + s * P, P)]).then_inc(x_in[s], 16)

            load(0, 0, True)
            load(0, 1, True)
            with sp.Fori(1, NT // 2) as i:
                load(i, 0, False)
                load(i, 1, False)

        @block.tensor
        def _(pe):
            pe.wait_ge(params_loaded, 64)

            def tile(i, s, first):
                pe.wait_ge(att_loaded[s], (i + 1) * 16)
                if not first:
                    pe.wait_ge(y_ready, 2 * i + s - 1)
                for k in range(KT):
                    mm = nc.tensor.matmul(ps[s][:, :], att[:, s, k], wo_sb[:, k], start=(k == 0),
                                          stop=(k == KT - 1))
                mm.then_inc(out_done, 1)

            tile(0, 0, True)
            tile(0, 1, True)
            with pe.Fori(1, NT // 2) as i:
                tile(i, 0, False)
                tile(i, 1, False)

        @block.gpsimd
        def _(pool):
            pool.wait_ge(params_loaded, 64)

            def add_bo(i, s, first):
                pool.wait_ge(x_in[s], (i + 1) * 16)
                if not first:
                    pool.wait_ge(y_ready, 2 * i + s - 1)
                nc.gpsimd.tensor_tensor(xb[:, s], xr[:, s], bo_sb[:, :], ALU.add).then_inc(xb_ready, 1)

            def add_ln_b(i, s, first):
                pool.wait_ge(yg_ready, 2 * i + s + 1)
                if not first:
                    pool.wait_ge(out_stored[s], i * 16)
                nc.gpsimd.tensor_tensor(yo[:, s], yg[:, s], b_sb[:, :], ALU.add).then_inc(yo_ready, 1)

            def pair(i, first):
                add_bo(i, 0, first)
                add_bo(i, 1, first)
                add_ln_b(i, 0, first)
                add_ln_b(i, 1, first)

            pair(0, True)
            with pool.Fori(1, NT // 2) as i:
                pair(i, False)

        @block.vector
        def _(dve):
            nc.vector.memset(eps[:, :], EPS).then_inc(eps_set, 1)
            dve.wait_ge(params_loaded, 64)

            def head(i, s, first):
                n = 2 * i + s
                dve.wait_ge(out_done, n + 1)
                dve.wait_ge(xb_ready, n + 1)
                if not first:
                    dve.wait_ge(yn_ready, n - 1)
                nc.vector.tensor_tensor(y[:, s], ps[s][:, :], xb[:, s], ALU.add).then_inc(y_ready, 1)
                dve.wait_ge(y_ready, n + 1)
                nc.vector.bn_stats(stats[:, s], y[:, s]).then_inc(stats_ready, 1)
                dve.wait_ge(params_loaded, 64)
                dve.wait_ge(stats_ready, n + 1)
                nc.vector.bn_aggr(mv[:, s], stats[:, s]).then_inc(mv_ready, 1)

            def middle(i, s):
                n = 2 * i + s
                dve.wait_ge(std_ready, n + 1)
                nc.vector.reciprocal(rstd[:, s], std[:, s]).then_inc(rstd_ready, 1)
                dve.wait_ge(rstd_ready, n + 1)
                nc.vector.scalar_tensor_tensor(out=nmean[:, s], in0=mv[:, s, 0:1], scalar=-1.0,
                                               in1=rstd[:, s], op0=ALU.mult,
                                               op1=ALU.mult).then_inc(nmean_ready, 1)

            def tail(i, s, first):
                n = 2 * i + s
                dve.wait_ge(yn_ready, n + 1)
                if not first:
                    dve.wait_ge(yo_ready, n - 1)
                nc.vector.tensor_tensor(yg[:, s], yn[:, s], g_sb[:, :], ALU.mult).then_inc(yg_ready, 1)

            def pair(i, first):
                head(i, 0, first)
                head(i, 1, first)
                middle(i, 0)
                middle(i, 1)
                tail(i, 0, first)
                tail(i, 1, first)

            pair(0, True)
            with dve.Fori(1, NT // 2) as i:
                pair(i, False)

        @block.scalar
        def _(act):
            act.wait_ge(eps_set, 1)

            def root(i, s):
                act.wait_ge(mv_ready, 2 * i + s + 1)
                nc.scalar.activation(std[:, s], mv[:, s, 1:2], ACT.Sqrt,
                                     bias=eps[:, :]).then_inc(std_ready, 1)

            def scale(i, s, first):
                n = 2 * i + s
                act.wait_ge(nmean_ready, n + 1)
                if not first:
                    act.wait_ge(yg_ready, n - 1)
                nc.scalar.activation(yn[:, s], y[:, s], ACT.Identity, bias=nmean[:, s],
                                     scale=rstd[:, s]).then_inc(yn_ready, 1)

            def store(i, s):
                act.wait_ge(yo_ready, 2 * i + s + 1)
                act.dma_start(out[bass.ds(i * (2 * P) + s * P, P)], yo[:, s]).then_inc(out_stored[s], 16)

            def pair(i, first):
                root(i, 0)
                root(i, 1)
                scale(i, 0, first)
                scale(i, 1, first)
                store(i, 0)
                store(i, 1)

            pair(0, True)
            with act.Fori(1, NT // 2) as i:
                pair(i, False)
            for s in range(2):
                act.wait_ge(out_stored[s], 16 * (NT // 2))


def kernel(x, ctx_4096, mask_BxS2_ik0, L0_xattn_Wq, L0_xattn_bq, L0_xattn_Wk, L0_xattn_bk,
           L0_xattn_Wv, L0_xattn_bv, L0_xattn_Wo, L0_xattn_bo, L0_xattn_ln_g, L0_xattn_ln_b):
    import numpy as np
    import concourse.bacc as bacc
    from concourse.bass_utils import run_bass_kernel_spmd

    def c(a):
        return np.ascontiguousarray(a)

    def weight(w):
        return c(np.asarray(w).T.reshape(KT, P, D).transpose(1, 0, 2).reshape(P, KT * D))

    def column(v):
        return c(np.asarray(v).reshape(KT, P).T)

    x = np.asarray(x)
    context = np.asarray(ctx_4096)
    rows = np.arange(P)
    head_mask = ((rows[:, None] % 64) // HD == np.arange(4)[None, :]).astype(np.float32)
    den_sel = ((rows[:, None] % 32 == HD) & (rows[:, None] // 32 == rows[None, :] // 32)).astype(np.float32)
    bv = np.asarray(L0_xattn_bv)
    bv_col = np.zeros((4, 32, NG * 2), bv.dtype)
    bv_col[:, 0:HD] = bv.reshape(NG * 2, 4, HD).transpose(1, 2, 0)

    arrays = {
        "ctxT": c(context.reshape(B, NP, SP_, KT, P).transpose(0, 1, 4, 3, 2)),
        "maskT": c(np.asarray(mask_BxS2_ik0).reshape(B, NC_, SC).transpose(0, 2, 1)),
        "xT": c(x.reshape(NQB, BPB * L, KT, P).transpose(0, 3, 2, 1)),
        "x_rows": c(x.reshape(ROWS, D)),
        "wqT": weight(L0_xattn_Wq), "wkT": weight(L0_xattn_Wk), "wvT": weight(L0_xattn_Wv),
        "woT": weight(L0_xattn_Wo),
        "bq": column(L0_xattn_bq), "bk": column(L0_xattn_bk), "bv_col": c(bv_col.reshape(P, NG * 2)),
        "bo": c(L0_xattn_bo), "ln_g": c(L0_xattn_ln_g), "ln_b": c(L0_xattn_ln_b),
        "ident": np.eye(P, dtype=np.float32), "head_mask": head_mask, "den_sel": den_sel,
    }
    nc = bacc.Bacc("TRN2", target_bir_lowering=False, num_devices=1)
    ap = {n: nc.dram_tensor(n, a.shape, mybir.dt.from_np(a.dtype), kind="ExternalInput").ap()
          for n, a in arrays.items()}
    q_scratch = nc.dram_tensor("q_scratch", (B, 64, NG, 2, L), F32, kind="Internal").ap()
    att_scratch = nc.dram_tensor("att_scratch", (NG * 2, 4, HD, B, L), F32, kind="Internal").ap()
    out = nc.dram_tensor("out", (ROWS, D), F32, kind="ExternalOutput").ap()
    build_attention(nc, ap["ctxT"], ap["maskT"], ap["xT"], ap["x_rows"], ap["wqT"], ap["wkT"],
                    ap["wvT"], ap["woT"], ap["bq"], ap["bk"], ap["bv_col"], ap["bo"], ap["ln_g"],
                    ap["ln_b"], ap["ident"], ap["head_mask"], ap["den_sel"], q_scratch,
                    att_scratch, out)
    build_output(nc, ap["x_rows"], ap["woT"], ap["bo"], ap["ln_g"], ap["ln_b"], att_scratch, out)
    r = run_bass_kernel_spmd(nc, [arrays], core_ids=[0])
    return r.results[0]["out"].reshape(B, L, D)
```

```python
from contextlib import ExitStack

import concourse.bass as bass
from concourse import mybir

F32 = mybir.dt.float32
F32R = mybir.dt.float32r
I32 = mybir.dt.int32
ALU = mybir.AluOpType
ACT = mybir.ActivationFunctionType
AX = mybir.AxisListType

P = 128
B, L, S, D = 32, 56, 1500, 512
NH, HD = 32, 16
KT = D // P
NG = 4
HG = NH // NG
SC = 125
NC_ = S // SC
NP = 6
SP_ = S // NP
NQ = 3
SQ = S // NQ
CQ = NC_ // NQ
NR = 3
NV = 3
DH = D // 2
HW = HG * L
HALF = HW // 2
VW = HD + 1
NQB = 4
BPB = B // NQB
ROWS = B * L
NT = ROWS // P
EPS = 1e-5
MASKED = -3.0e38
FLOOR = -1.0e38
MQ = HW // 4


def build_attention(nc, ctxT, maskT, xT, x_rows, wqT, wkT, wvT, woT, bq, bk, bv_col, bo, ln_g,
                    ln_b, ident_in, head_mask_in, den_sel_in, q_scratch, att_scratch, out):
    with ExitStack() as ctx:
        def sb(name, shape, dt=F32):
            return ctx.enter_context(nc.sbuf_tensor(name + "_sb", shape, dt))

        def psum(name, shape):
            return ctx.enter_context(nc.psum_tensor(name, shape, F32))

        def sem(name):
            return ctx.enter_context(nc.semaphore(name))

        s_buf = sb("s_buf", [P, 2, NC_, HW])
        wk_hi = sb("wk_hi", [P, KT, D], F32R)
        wk_lo = sb("wk_lo", [P, KT, D], F32R)
        wv_hi = sb("wv_hi", [P, KT, D], F32R)
        wv_lo = sb("wv_lo", [P, KT, D], F32R)
        c_hi = sb("c_hi", [P, KT, S], F32R)
        c_lo = sb("c_lo", [P, KT, S], F32R)
        raw = sb("raw", [P, NR, KT, SP_])
        k_a = sb("k_a", [P, S], F32R)
        k_b = sb("k_b", [P, S], F32R)
        v_sb = sb("v_sb", [P, NC_, NH, VW])
        qd_hi = sb("qd_hi", [P, 2, 2, HALF], F32R)
        qd_lo = sb("qd_lo", [P, 2, 2, HALF], F32R)
        q_raw = sb("q_raw", [P, NG, 2, L])
        q_hi = sb("q_hi", [P, NG, 2, L], F32R)
        q_lo = sb("q_lo", [P, NG, 2, L])
        mx = sb("mx", [P, 2, HW])
        mx_one = sb("mx_one", [P, HW])
        col_max = sb("col_max", [MQ, 4])
        diag_hi = sb("diag_hi", [MQ, 4, MQ], F32R)
        diag_lo = sb("diag_lo", [MQ, 4, MQ], F32R)
        col_hi = sb("col_hi", [MQ, 4], F32R)
        col_lo = sb("col_lo", [MQ, 4])
        mask_i = sb("mask_i", [P, NC_], I32)
        mask_bias = sb("mask_bias", [P, NC_])
        o_raw = sb("o_raw", [P, 2 * L])
        o_rec = sb("o_rec", [P, 2 * L])
        o_mul = sb("o_mul", [P, 2 * L])
        o_out = sb("o_out", [P, NG, 2, L])
        ident = sb("ident", [P, P])
        ones = sb("ones", [P, P], F32R)
        head_mask = sb("head_mask", [P, 4])
        den_sel = sb("den_sel", [P, P])
        bq_sb = sb("bq_sb", [P, KT])
        bq_scaled = sb("bq_scaled", [P, KT])
        bk_sb = sb("bk_sb", [P, KT])
        bv_sb = sb("bv_sb", [P, NG, 2])

        stage = s_buf[:, :, :, :].rearrange("p a c n -> p (a c n)")
        wk_raw = stage[:, 0:KT * D]
        wv_raw = stage[:, KT * D:2 * KT * D]
        wq_raw = stage[:, 2 * KT * D:3 * KT * D].rearrange("p (k n) -> p k n", k=KT)
        NX = BPB * L
        x_at = 3 * KT * D
        x_raw = stage[:, x_at:x_at + 2 * KT * NX].rearrange("p (s k n) -> p s k n", s=2, k=KT)
        q_stage = v_sb[:, :, :, :].rearrange("p c h w -> p (c h w)")[:, 0:4 * NX].rearrange(
            "p (s n) -> p s n", s=4)

        ps_k = psum("ps_k", [P, 512])
        ps_v = psum("ps_v", [P, 512])
        ps_score = [psum(f"ps_score{i}", [P, 512]) for i in range(4)]
        ps_o = psum("ps_o", [P, 512])
        ps_max = psum("ps_max", [P, 512])

        weights_loaded = sem("weights_loaded")
        wq_loaded = sem("wq_loaded")
        consts_loaded = sem("consts_loaded")
        x_loaded = [sem(f"x_loaded{i}") for i in range(2)]
        weights_split_hi = sem("weights_split_hi")
        weights_split_lo = sem("weights_split_lo")
        memsets_done = sem("memsets_done")
        bq_ready = sem("bq_ready")
        qproj_done = sem("qproj_done")
        q_evicted = sem("q_evicted")
        q_stored = [sem(f"q_stored{i}") for i in range(4)]
        raw_loaded = [sem(f"raw_loaded{i}") for i in range(NR)]
        batch_loaded = sem("batch_loaded")
        c_hi_ready = sem("c_hi_ready")
        c_lo_ready = sem("c_lo_ready")
        q_hi_ready = sem("q_hi_ready")
        q_lo_ready = sem("q_lo_ready")
        qd_ready = sem("qd_ready")
        mask_ready = sem("mask_ready")
        kproj_done = sem("kproj_done")
        k_hi_ready = sem("k_hi_ready")
        k_lo_ready = sem("k_lo_ready")
        vproj_done = sem("vproj_done")
        v_ready = sem("v_ready")
        scores_done = sem("scores_done")
        s_ready = sem("s_ready")
        max_step = sem("max_step")
        maxT_done = sem("maxT_done")
        colmax_ready = sem("colmax_ready")
        colhi_ready = sem("colhi_ready")
        collo_ready = sem("collo_ready")
        diag_ready = sem("diag_ready")
        spread_done = sem("spread_done")
        shifted = sem("shifted")
        exp_done = sem("exp_done")
        pv_done = sem("pv_done")
        o_raw_ready = sem("o_raw_ready")
        den_done = sem("den_done")
        rec_ready = sem("rec_ready")
        mul_ready = sem("mul_ready")
        o_ready = sem("o_ready")
        att_stored = sem("att_stored")

        NMAX = 6
        SH = 4
        NSH = NC_ // SH
        QDMA = 32
        BATCH_DMA = QDMA + 16

        block = ctx.enter_context(nc.Block())

        @block.sync
        def _(sp):
            sp.dma_start(wq_raw, wqT.rearrange("p (k n) -> p k n", k=KT)).then_inc(wq_loaded, 16)
            sp.dma_start(x_raw[:, 0], xT[0]).then_inc(x_loaded[0], 16)
            for dst, src in ((ident[:, :], ident_in), (head_mask[:, :], head_mask_in),
                             (den_sel[:, :], den_sel_in), (bq_sb[:, :], bq), (bk_sb[:, :], bk),
                             (bv_sb[:, :, :], bv_col.rearrange("p (g s) -> p g s", g=NG))):
                sp.dma_start(dst, src).then_inc(consts_loaded, 16)
            sp.dma_start(x_raw[:, 1], xT[1]).then_inc(x_loaded[1], 16)
            sp.dma_start(wk_raw, wkT).then_inc(weights_loaded, 16)
            sp.dma_start(wv_raw, wvT).then_inc(weights_loaded, 16)

            def load_piece(b, i, first):
                if not (first and i < NR):
                    sp.wait_ge(c_hi_ready, b * NP + (i + 1 - NR))
                    sp.wait_ge(c_lo_ready, b * NP + (i + 1 - NR))
                sp.dma_start(raw[:, i % NR], ctxT[bass.ds(b, 1), i].rearrange(
                    "o p k n -> (o p) k n")).then_inc(raw_loaded[i % NR], 16)

            def load_queries(b, first):
                if not first:
                    sp.wait_ge(q_lo_ready, b)
                    sp.wait_ge(mask_ready, b)
                for half in range(2):
                    sp.dma_start(q_raw[64 * half:64 * half + 64], q_scratch[bass.ds(b, 1)].rearrange(
                        "o p g s l -> (o p) g s l")).then_inc(batch_loaded, 16)
                sp.dma_start(mask_i[0:SC, :], maskT[bass.ds(b, 1)].rearrange(
                    "o p c -> (o p) c")).then_inc(batch_loaded, 16)

            def store_attention(b):
                sp.wait_ge(o_ready, (b + 1) * NG)
                for j in range(4):
                    sp.dma_start(
                        att_scratch[:, j, :, bass.ds(b, 1)].rearrange("s d o l -> d s (o l)"),
                        o_out[32 * j:32 * j + HD].rearrange("p g s l -> p (g s) l"),
                    ).then_inc(att_stored, 16)

            for i in range(NR):
                load_piece(0, i, True)
            for n in range(NQB):
                for g in range(NG):
                    i = n * NG + g
                    sp.wait_ge(q_evicted, i + 1)
                    for s in range(2):
                        sp.dma_start(
                            q_scratch[n * BPB:(n + 1) * BPB, :, g, s].rearrange("b p l -> p b l"),
                            q_stage[64 * s:64 * s + 64, i % 4].rearrange("p (b l) -> p b l", b=BPB),
                        ).then_inc(q_stored[i % 4], 16)
                if n + 2 < NQB:
                    sp.wait_ge(qproj_done, (n + 1) * NG)
                    sp.dma_start(x_raw[:, n % 2], xT[n + 2]).then_inc(x_loaded[n % 2], 16)
                if n == 0:
                    for i in range(4):
                        sp.wait_ge(q_stored[i], 32)
                    load_queries(0, True)
                if n == 2:
                    for i in range(NR, NP):
                        load_piece(0, i, True)
            for i in range(4):
                sp.wait_ge(q_stored[i], 32 * NQB)
            for i in range(NP):
                if i == NR:
                    load_queries(1, False)
                load_piece(1, i, False)
            with sp.Fori(1, B - 1) as b:
                store_attention(b - 1)
                for i in range(NP):
                    if i == NR:
                        load_queries(b + 1, False)
                    load_piece(b + 1, i, False)
            store_attention(B - 2)
            store_attention(B - 1)
            sp.wait_ge(att_stored, 64 * B)

        @block.tensor
        def _(pe):
            pe.wait_ge(wq_loaded, 16)
            for n in range(NQB):
                pe.wait_ge(x_loaded[n % 2], 16 * (n // 2 + 1))
                for g in range(NG):
                    i = n * NG + g
                    if i >= 4:
                        pe.wait_ge(q_evicted, i - 3)
                    for k in range(KT):
                        mm = nc.tensor.matmul(ps_score[i % 4][:, 0:NX], wq_raw[:, k, g * P:(g + 1) * P],
                                              x_raw[:, n % 2, k], start=(k == 0), stop=(k == KT - 1))
                    mm.then_inc(qproj_done, 1)
            pe.wait_ge(consts_loaded, 96)
            pe.wait_ge(memsets_done, 3)
            pe.wait_ge(weights_split_hi, 2)
            pe.wait_ge(weights_split_lo, 2)

            def project_k(t, b, g, q, first, between=None):
                if g == 0:
                    pe.wait_ge(c_hi_ready, b * NP + 2 * q + 2)
                    pe.wait_ge(c_lo_ready, b * NP + 2 * q + 2)
                if not (first and g == 0 and q == 0):
                    pe.wait_ge(k_lo_ready, t * NQ + q)
                bank = ps_k[:, 0:SQ]
                keys = slice(q * SQ, (q + 1) * SQ)
                cols = slice(g * P, (g + 1) * P)
                for k in range(KT):
                    if k == 2 and between is not None:
                        max_transposes(between)
                    nc.tensor.matmul(bank, wk_hi[:, k, cols], c_hi[:, k, keys], start=(k == 0), stop=False)
                    nc.tensor.matmul(bank, wk_hi[:, k, cols], c_lo[:, k, keys], start=False, stop=False)
                    mm = nc.tensor.matmul(bank, wk_lo[:, k, cols], c_hi[:, k, keys], start=False,
                                          stop=(k == KT - 1))
                mm.then_inc(kproj_done, 1)

            def project_v(t, g, n, first):
                if not (first and g == 0 and n == 0):
                    pe.wait_ge(v_ready, t * NV + n)
                half = slice((g // 2) * DH, (g // 2 + 1) * DH)
                for c in range(2):
                    at = ((g % 2) * 2 * NV + 2 * n + c) * SC
                    keys = slice(at, at + SC)
                    bank = ps_v[0:SC, c * DH:(c + 1) * DH]
                    for k in range(KT):
                        hi, lo = c_hi[:, k, keys], c_lo[:, k, keys]
                        nc.tensor.matmul(bank, hi, wv_hi[:, k, half], start=(k == 0), stop=False)
                        nc.tensor.matmul(bank, hi, wv_lo[:, k, half], start=False, stop=False)
                        mm = nc.tensor.matmul(bank, lo, wv_hi[:, k, half], start=False,
                                              stop=(k == KT - 1))
                mm.then_inc(vproj_done, 1)

            def scores(t, g, first):
                pe.wait_ge(qd_ready, t + 1)
                for c in range(NC_):
                    if c % CQ == 0:
                        pe.wait_ge(k_hi_ready, 2 * (t * NQ + c // CQ + 1))
                        pe.wait_ge(k_lo_ready, t * NQ + c // CQ + 1)
                    if not (first and g == 0 and c < 4):
                        pe.wait_ge(s_ready, t * NC_ + c - 3)
                    bank = ps_score[c % 4]
                    for s, kk in enumerate((k_a, k_b)):
                        w = kk[:, c * SC:(c + 1) * SC]
                        o = bank[0:SC, s * HALF:(s + 1) * HALF]
                        nc.tensor.matmul(o, w, qd_hi[:, g % 2, s], start=True, stop=False)
                        mm = nc.tensor.matmul(o, w, qd_lo[:, g % 2, s], start=False, stop=True)
                    mm.then_inc(scores_done, 1)

            def max_transposes(t):
                pe.wait_ge(max_step, (t + 1) * NMAX)
                if not (isinstance(t, int) and t == 0):
                    pe.wait_ge(shifted, t * NSH)
                for i in range(4):
                    mm = nc.tensor.transpose(ps_max[0:MQ, i * SC:(i + 1) * SC],
                                             mx_one[0:SC, i * MQ:(i + 1) * MQ], ident[0:SC, 0:SC])
                mm.then_inc(maxT_done, 1)

            def max_spread(t):
                pe.wait_ge(diag_ready, t + 1)
                top = ps_max[0:SC, 0:HW]
                nc.tensor.matmul(top, ones[0:MQ, 0:SC], diag_hi[:, :, :].rearrange("p a n -> p (a n)"),
                                 start=True, stop=False)
                nc.tensor.matmul(top, ones[0:MQ, 0:SC], diag_lo[:, :, :].rearrange("p a n -> p (a n)"),
                                 start=False, stop=True).then_inc(spread_done, 1)

            def times_v(t, g):
                if not (isinstance(t, int) and t == 0):
                    pe.wait_ge(o_raw_ready, t)
                    pe.wait_ge(rec_ready, t)
                if g % 2 == 0:
                    pe.wait_ge(v_ready, (t + 2) * NV)
                for c in range(NC_):
                    if c % SH == 0:
                        pe.wait_ge(exp_done, t * NSH + c // SH + 1)
                    for s in range(2):
                        for j in range(4):
                            hh = 4 * s + j
                            mm = nc.tensor.matmul(
                                ps_o[32 * j:32 * j + VW, s * L:(s + 1) * L],
                                v_sb[0:SC, c, g * HG + hh], s_buf[0:SC, g % 2, c, hh * L:(hh + 1) * L],
                                start=(c == 0 and s == 0), stop=(c == NC_ - 1 and s == 1),
                                skip_group_check=True)
                mm.then_inc(pv_done, 1)

            def denominators(t):
                pe.wait_ge(o_raw_ready, t + 1)
                nc.tensor.matmul(ps_o[:, 2 * L:4 * L], den_sel[:, :], o_raw[:, :], start=True,
                                 stop=True, skip_group_check=True).then_inc(den_done, 1)

            def step(b, g, first):
                t = b * NG + g
                begun = not (first and g == 0)
                ended = not (first and g < 2)
                project_k(t, b, g, 0, first)
                project_v(t, g, 0, first)
                project_k(t, b, g, 1, first, between=t - 1 if begun else None)
                project_v(t, g, 1, first)
                if begun:
                    max_spread(t - 1)
                project_k(t, b, g, 2, first)
                project_v(t, g, 2, first)
                if ended:
                    times_v(t - 2, (g - 2) % NG)
                scores(t, g, first)
                if ended:
                    denominators(t - 2)

            for g in range(NG):
                step(0, g, True)
            with pe.Fori(1, B) as b:
                for g in range(NG):
                    step(b, g, False)
            last = B * NG - 1
            times_v(last - 1, NG - 2)
            max_transposes(last)
            max_spread(last)
            denominators(last - 1)
            times_v(last, NG - 1)
            denominators(last)

        @block.scalar
        def _(act):
            def split_hi(b, i, first):
                act.wait_ge(raw_loaded[i % NR], (b * 2 + i // NR + 1) * 16)
                if not first:
                    act.wait_ge(kproj_done, (b * NG - 1) * NQ + i // 2 + 1)
                    if i >= NV:
                        act.wait_ge(vproj_done, (b * NG - 1) * NV + i - NV + 1)
                nc.scalar.copy(c_hi[:, :, i * SP_:(i + 1) * SP_], raw[:, i % NR]).then_inc(c_hi_ready, 1)

            act.wait_ge(consts_loaded, 96)
            nc.scalar.mul(bq_scaled[:, :], bq_sb[:, :], HD ** -0.5).then_inc(bq_ready, 1)
            act.wait_ge(bq_ready, 1)
            for i in range(NQB * NG):
                if i == 4:
                    act.wait_ge(weights_loaded, 32)
                    nc.scalar.copy(wk_hi[:, :, :].rearrange("p k n -> p (k n)"), wk_raw).then_inc(weights_split_hi, 1)
                if i == 5:
                    nc.scalar.copy(wv_hi[:, :, :].rearrange("p k n -> p (k n)"), wv_raw).then_inc(weights_split_hi, 1)
                if i >= 6 and i % 2 == 0 and i < 12:
                    split_hi(0, (i - 6) // 2, True)
                act.wait_ge(qproj_done, i + 1)
                if i >= 4:
                    act.wait_ge(q_stored[i % 4], 32 * (i // 4))
                nc.scalar.activation(q_stage[:, i % 4], ps_score[i % 4][:, 0:NX], ACT.Identity,
                                     bias=bq_scaled[:, i % NG:i % NG + 1],
                                     scale=HD ** -0.5).then_inc(q_evicted, 1)
            def round_queries(b):
                act.wait_ge(batch_loaded, (b + 1) * BATCH_DMA)
                if not (isinstance(b, int) and b == 0):
                    act.wait_ge(qd_ready, b * NG)
                nc.scalar.copy(q_hi[:, :, :, :], q_raw[:, :, :, :]).then_inc(q_hi_ready, 1)

            def evict_k_hi(t, g, q, first):
                act.wait_ge(kproj_done, t * NQ + q + 1)
                if not (first and g == 0) and q == 0:
                    act.wait_ge(scores_done, t * NC_)
                cols = slice(q * SQ, (q + 1) * SQ)
                bank = ps_k
                nc.scalar.activation(k_a[0:64, cols], bank[0:64, 0:SQ], ACT.Identity,
                                     bias=bk_sb[0:64, g:g + 1]).then_inc(k_hi_ready, 1)
                nc.scalar.activation(k_b[64:128, cols], bank[64:128, 0:SQ], ACT.Identity,
                                     bias=bk_sb[64:128, g:g + 1]).then_inc(k_hi_ready, 1)

            def exps(t, g, i):
                act.wait_ge(shifted, t * NSH + i + 1)
                part = s_buf[0:SC, g % 2, i * SH:(i + 1) * SH]
                nc.scalar.activation(part, part, ACT.Exp).then_inc(exp_done, 1)

            def evict_v(t, g, n, first):
                act.wait_ge(vproj_done, t * NV + n + 1)
                if not first and g % 2 == 0 and n == 0:
                    act.wait_ge(pv_done, t - 2)
                c = (g % 2) * 2 * NV + 2 * n
                heads = slice((g // 2) * (NH // 2), (g // 2 + 1) * (NH // 2))
                nc.scalar.copy(v_sb[0:SC, c:c + 2, heads, 0:HD], ps_v[0:SC, :].rearrange(
                    "p (c h d) -> p c h d", c=2, d=HD)).then_inc(v_ready, 1)

            def evict_scores(t, b, g, first):
                if g == 0:
                    act.wait_ge(mask_ready, b + 1)
                if not (first and g < 2):
                    act.wait_ge(pv_done, t - 1)
                for c in range(NC_):
                    act.wait_ge(scores_done, t * NC_ + c + 1)
                    nc.scalar.activation(s_buf[0:SC, g % 2, c], ps_score[c % 4][0:SC, 0:HW],
                                         ACT.Identity, bias=mask_bias[0:SC, c:c + 1]).then_inc(s_ready, 1)

            for i in range(NR, NP):
                split_hi(0, i, True)
            round_queries(0)

            def step(b, g, first, last):
                t = b * NG + g
                begun = not (first and g == 0)
                if g == 0 and not first:
                    split_hi(b, 4, False)
                    split_hi(b, 5, False)
                evict_k_hi(t, g, 0, first)
                evict_v(t, g, 0, first)
                if g == 3 and not last:
                    round_queries(b + 1)
                    split_hi(b + 1, 0, False)
                    split_hi(b + 1, 1, False)
                evict_k_hi(t, g, 1, first)
                evict_v(t, g, 1, first)
                if g == 3 and not last:
                    split_hi(b + 1, 2, False)
                if begun:
                    exps(t - 1, (g - 1) % NG, 0)
                evict_k_hi(t, g, 2, first)
                if g == 3 and not last:
                    split_hi(b + 1, 3, False)
                if begun:
                    exps(t - 1, (g - 1) % NG, 1)
                evict_v(t, g, 2, first)
                if begun:
                    exps(t - 1, (g - 1) % NG, 2)
                evict_scores(t, b, g, first)

            act.wait_ge(weights_split_lo, 2)
            act.wait_ge(memsets_done, 3)
            for g in range(NG):
                step(0, g, True, False)
            with act.Fori(1, B - 1) as b:
                for g in range(NG):
                    step(b, g, False, False)
            for g in range(NG):
                step(B - 1, g, False, True)
            for i in range(NSH):
                exps(B * NG - 1, NG - 1, i)

        @block.vector
        def _(dve):
            nc.vector.memset(ps_o[:, :], 0.0).then_inc(memsets_done, 1)
            nc.vector.memset(ones[:, :].bitcast(F32), 1.0).then_inc(memsets_done, 1)
            for hi, lo, w, n in ((wk_hi, wk_lo, wk_raw, 1), (wv_hi, wv_lo, wv_raw, 2)):
                dve.wait_ge(weights_split_hi, n)
                nc.vector.tensor_tensor(lo[:, :, :].rearrange("p k n -> p (k n)"), w,
                                        hi[:, :, :].rearrange("p k n -> p (k n)").bitcast(F32),
                                        ALU.subtract).then_inc(weights_split_lo, 1)
            for i in range(4):
                dve.wait_ge(q_stored[i], 32 * NQB)
            nc.vector.memset(v_sb[:, :, :, HD:VW], 1.0).then_inc(memsets_done, 1)

            def evict_k_lo(t, g, q):
                dve.wait_ge(k_hi_ready, 2 * (t * NQ + q) + 1)
                cols = slice(q * SQ, (q + 1) * SQ)
                bank = ps_k
                nc.vector.scalar_tensor_tensor(
                    out=k_a[64:128, cols], in0=bank[0:64, 0:SQ], scalar=bk_sb[0:64, g:g + 1],
                    in1=k_a[0:64, cols].bitcast(F32), op0=ALU.add, op1=ALU.subtract)
                dve.wait_ge(k_hi_ready, 2 * (t * NQ + q) + 2)
                nc.vector.scalar_tensor_tensor(
                    out=k_b[0:64, cols], in0=bank[64:128, 0:SQ], scalar=bk_sb[64:128, g:g + 1],
                    in1=k_b[64:128, cols].bitcast(F32), op0=ALU.add, op1=ALU.subtract).then_inc(k_lo_ready, 1)

            def chunk_max(t, g, first):
                part = s_buf[0:SC, g % 2]
                acc = mx[0:SC]
                for i in range(5):
                    dve.wait_ge(s_ready, t * NC_ + 2 * i + 4)
                    if i:
                        dve.wait_ge(max_step, t * NMAX + i)
                    nc.vector.tensor_tensor(acc, part[:, 2 * i + 2:2 * i + 4], acc if i else part[:, 0:2],
                                            ALU.max).then_inc(max_step, 1)

            def last_max(t):
                acc = mx[0:SC]
                if not (isinstance(t, int) and t == 0):
                    dve.wait_ge(maxT_done, t)
                dve.wait_ge(max_step, t * NMAX + 5)
                nc.vector.scalar_tensor_tensor(out=mx_one[0:SC], in0=acc[:, 0], scalar=FLOOR, in1=acc[:, 1],
                                               op0=ALU.max, op1=ALU.max).then_inc(max_step, 1)

            def mask_to_bias(b):
                dve.wait_ge(batch_loaded, (b + 1) * BATCH_DMA)
                if not (isinstance(b, int) and b == 0):
                    dve.wait_ge(s_ready, b * NG * NC_)
                nc.vector.tensor_scalar(mask_bias[0:SC, :], mask_i[0:SC, :], 0, MASKED, ALU.is_equal,
                                        ALU.mult).then_inc(mask_ready, 1)

            def partition_max(t):
                dve.wait_ge(maxT_done, t + 1)
                nc.vector.tensor_reduce(col_max[:, :], ps_max[0:MQ, 0:4 * SC].rearrange(
                    "p (a n) -> p a n", a=4), AX.X, ALU.max).then_inc(colmax_ready, 1)
                dve.wait_ge(colmax_ready, t + 1)
                nc.vector.tensor_copy(col_hi[:, :], col_max[:, :]).then_inc(colhi_ready, 1)
                for dst, src in ((diag_hi, col_hi[:, :].bitcast(F32)), (diag_lo, col_lo[:, :])):
                    if dst is diag_hi:
                        dve.wait_ge(colhi_ready, t + 1)
                        nc.vector.tensor_tensor(col_lo[:, :], col_max[:, :], src,
                                                ALU.subtract).then_inc(collo_ready, 1)
                    else:
                        dve.wait_ge(collo_ready, t + 1)
                    ins = nc.vector.tensor_tensor(
                        dst[:, :, :], ident[0:MQ, 0:MQ].unsqueeze(1).to_broadcast([MQ, 4, MQ]),
                        src.unsqueeze(2).to_broadcast([MQ, 4, MQ]), ALU.mult)
                ins.then_inc(diag_ready, 1)

            def shift(t, g):
                dve.wait_ge(spread_done, t + 1)
                top = ps_max[0:SC, 0:HW].unsqueeze(1).to_broadcast([SC, SH, HW])
                for i in range(NSH):
                    part = s_buf[0:SC, g % 2, i * SH:(i + 1) * SH]
                    nc.vector.tensor_tensor(part, part, top, ALU.subtract).then_inc(shifted, 1)

            def take_output(t):
                dve.wait_ge(pv_done, t + 1)
                if not (isinstance(t, int) and t == 0):
                    dve.wait_ge(mul_ready, t)
                nc.vector.tensor_copy(o_raw[:, :], ps_o[:, 0:2 * L]).then_inc(o_raw_ready, 1)

            def normalise(t, g, b):
                dve.wait_ge(den_done, t + 1)
                nc.vector.reciprocal(o_rec[:, :], ps_o[:, 2 * L:4 * L]).then_inc(rec_ready, 1)
                dve.wait_ge(rec_ready, t + 1)
                nc.vector.tensor_tensor(o_mul[:, :], o_raw[:, :], o_rec[:, :], ALU.mult).then_inc(mul_ready, 1)
                dve.wait_ge(mul_ready, t + 1)
                if g == 0 and not (isinstance(b, int) and b == 0):
                    dve.wait_ge(att_stored, b * 64)
                nc.vector.tensor_tensor(
                    o_out[:, g], o_mul[:, :].rearrange("p (s l) -> p s l", s=2),
                    bv_sb[:, g].unsqueeze(2).to_broadcast([P, 2, L]), ALU.add).then_inc(o_ready, 1)

            def step(b, g, first, last):
                t = b * NG + g
                begun = not (first and g == 0)
                ended = not (first and g < 2)
                evict_k_lo(t, g, 0)
                if begun:
                    last_max(t - 1)
                if not (first and g < 3):
                    normalise(t - 3, (g - 3) % NG, b if g == 3 else b - 1)
                if begun:
                    partition_max(t - 1)
                evict_k_lo(t, g, 1)
                if begun:
                    shift(t - 1, (g - 1) % NG)
                evict_k_lo(t, g, 2)
                if ended:
                    take_output(t - 2)
                chunk_max(t, g, first)
                if g == 3 and not last:
                    mask_to_bias(b + 1)

            mask_to_bias(0)
            for g in range(NG):
                step(0, g, True, False)
            with dve.Fori(1, B - 1) as b:
                for g in range(NG):
                    step(b, g, False, False)
            for g in range(NG):
                step(B - 1, g, False, True)
            last = B * NG - 1
            last_max(last)
            normalise(last - 2, NG - 3, B - 1)
            take_output(last - 1)
            partition_max(last)
            shift(last, NG - 1)
            normalise(last - 1, NG - 2, B - 1)
            take_output(last)
            normalise(last, NG - 1, B - 1)

        @block.gpsimd
        def _(pool):
            def split_lo(b, i):
                pool.wait_ge(c_hi_ready, b * NP + i + 1)
                keys = slice(i * SP_, (i + 1) * SP_)
                nc.gpsimd.tensor_tensor(c_lo[:, :, keys], raw[:, i % NR], c_hi[:, :, keys].bitcast(F32),
                                        ALU.subtract).then_inc(c_lo_ready, 1)

            def split_queries(b):
                pool.wait_ge(q_hi_ready, b + 1)
                nc.gpsimd.tensor_tensor(q_lo[:, :, :, :], q_raw[:, :, :, :], q_hi[:, :, :, :].bitcast(F32),
                                        ALU.subtract).then_inc(q_lo_ready, 1)

            def query_blocks(t, b, g, first):
                if not (first and g < 2):
                    pool.wait_ge(scores_done, (t - 1) * NC_)
                pool.wait_ge(q_lo_ready, b + 1)
                for dst, src in ((qd_hi, q_hi), (qd_lo, q_lo)):
                    for s in range(2):
                        q = src[:, g, s] if src is q_lo else src[:, g, s].bitcast(F32)
                        last = nc.gpsimd.tensor_tensor(
                            dst[:, g % 2, s].rearrange("p (h l) -> p h l", h=4),
                            q.unsqueeze(1).to_broadcast([P, 4, L]),
                            head_mask[:, :].unsqueeze(2).to_broadcast([P, 4, L]), ALU.mult)
                last.then_inc(qd_ready, 1)

            pool.wait_ge(consts_loaded, 96)
            for i in range(NP):
                split_lo(0, i)
            split_queries(0)
            query_blocks(0, 0, 0, True)

            def step(b, g, first, last):
                t = b * NG + g
                if g == 0 and not first:
                    split_lo(b, 4)
                    split_lo(b, 5)
                if g < 3:
                    query_blocks(t + 1, b, g + 1, first)
                elif not last:
                    split_queries(b + 1)
                    query_blocks(t + 1, b + 1, 0, False)
                    for i in range(4):
                        split_lo(b + 1, i)

            for g in range(NG):
                step(0, g, True, False)
            with pool.Fori(1, B - 1) as b:
                for g in range(NG):
                    step(b, g, False, False)
            for g in range(NG):
                step(B - 1, g, False, True)


def build_output(nc, x_rows, woT, bo, ln_g, ln_b, att_scratch, out):
    with ExitStack() as ctx:
        def sb(name, shape):
            return ctx.enter_context(nc.sbuf_tensor(name + "_sb", shape, F32))

        def sem(name):
            return ctx.enter_context(nc.semaphore(name))

        wo_sb = sb("wo_sb", [P, KT, D])
        bo_sb = sb("bo_sb", [P, D])
        g_sb = sb("g_sb", [P, D])
        b_sb = sb("b_sb", [P, D])
        eps = sb("eps", [P, 1])
        att = sb("att", [P, 2, KT, P])
        xr = sb("xr", [P, 2, D])
        xb = sb("xb", [P, 2, D])
        y = sb("y", [P, 2, D])
        yn = sb("yn", [P, 2, D])
        yg = sb("yg", [P, 2, D])
        yo = sb("yo", [P, 2, D])
        stats = sb("stats", [P, 2, 6])
        mv = sb("mv", [P, 2, 2])
        std = sb("std", [P, 2, 1])
        rstd = sb("rstd", [P, 2, 1])
        nmean = sb("nmean", [P, 2, 1])
        ps = [ctx.enter_context(nc.psum_tensor(f"ps_out{i}", [P, 512], F32)) for i in range(2)]

        params_loaded = sem("params_loaded")
        att_loaded = [sem(f"att_loaded{i}") for i in range(2)]
        x_in = [sem(f"x_in{i}") for i in range(2)]
        eps_set = sem("eps_set")
        xb_ready = sem("xb_ready")
        out_done = sem("out_done")
        y_ready = sem("y_ready")
        stats_ready = sem("stats_ready")
        mv_ready = sem("mv_ready")
        std_ready = sem("std_ready")
        rstd_ready = sem("rstd_ready")
        nmean_ready = sem("nmean_ready")
        yn_ready = sem("yn_ready")
        yg_ready = sem("yg_ready")
        yo_ready = sem("yo_ready")
        out_stored = [sem(f"out_stored{i}") for i in range(2)]

        block = ctx.enter_context(nc.Block())
        attT = att_scratch.rearrange("(k s) j d b l -> k (s j d) (b l)", k=KT)

        @block.sync
        def _(sp):
            for dst, src in ((wo_sb[:, :, :], woT.rearrange("p (k n) -> p k n", k=KT)),
                             (bo_sb[:, :], bo.partition_broadcast(P)),
                             (g_sb[:, :], ln_g.partition_broadcast(P)),
                             (b_sb[:, :], ln_b.partition_broadcast(P))):
                sp.dma_start(dst, src).then_inc(params_loaded, 16)

            def load(i, s, first):
                if not first:
                    sp.wait_ge(out_done, 2 * i + s - 1)
                    sp.wait_ge(xb_ready, 2 * i + s - 1)
                sp.dma_start(att[:, s], attT[:, :, bass.ds(i * (2 * P) + s * P, P)].rearrange(
                    "k p n -> p k n")).then_inc(att_loaded[s], 16)
                sp.dma_start(xr[:, s], x_rows[bass.ds(i * (2 * P) + s * P, P)]).then_inc(x_in[s], 16)

            load(0, 0, True)
            load(0, 1, True)
            with sp.Fori(1, NT // 2) as i:
                load(i, 0, False)
                load(i, 1, False)

        @block.tensor
        def _(pe):
            pe.wait_ge(params_loaded, 64)

            def tile(i, s, first):
                pe.wait_ge(att_loaded[s], (i + 1) * 16)
                if not first:
                    pe.wait_ge(y_ready, 2 * i + s - 1)
                for k in range(KT):
                    mm = nc.tensor.matmul(ps[s][:, :], att[:, s, k], wo_sb[:, k], start=(k == 0),
                                          stop=(k == KT - 1))
                mm.then_inc(out_done, 1)

            tile(0, 0, True)
            tile(0, 1, True)
            with pe.Fori(1, NT // 2) as i:
                tile(i, 0, False)
                tile(i, 1, False)

        @block.gpsimd
        def _(pool):
            pool.wait_ge(params_loaded, 64)

            def add_bo(i, s, first):
                pool.wait_ge(x_in[s], (i + 1) * 16)
                if not first:
                    pool.wait_ge(y_ready, 2 * i + s - 1)
                nc.gpsimd.tensor_tensor(xb[:, s], xr[:, s], bo_sb[:, :], ALU.add).then_inc(xb_ready, 1)

            def add_ln_b(i, s, first):
                pool.wait_ge(yg_ready, 2 * i + s + 1)
                if not first:
                    pool.wait_ge(out_stored[s], i * 16)
                nc.gpsimd.tensor_tensor(yo[:, s], yg[:, s], b_sb[:, :], ALU.add).then_inc(yo_ready, 1)

            def pair(i, first):
                add_bo(i, 0, first)
                add_bo(i, 1, first)
                add_ln_b(i, 0, first)
                add_ln_b(i, 1, first)

            pair(0, True)
            with pool.Fori(1, NT // 2) as i:
                pair(i, False)

        @block.vector
        def _(dve):
            nc.vector.memset(eps[:, :], EPS).then_inc(eps_set, 1)
            dve.wait_ge(params_loaded, 64)

            def head(i, s, first):
                n = 2 * i + s
                dve.wait_ge(out_done, n + 1)
                dve.wait_ge(xb_ready, n + 1)
                if not first:
                    dve.wait_ge(yn_ready, n - 1)
                nc.vector.tensor_tensor(y[:, s], ps[s][:, :], xb[:, s], ALU.add).then_inc(y_ready, 1)
                dve.wait_ge(y_ready, n + 1)
                nc.vector.bn_stats(stats[:, s], y[:, s]).then_inc(stats_ready, 1)
                dve.wait_ge(params_loaded, 64)
                dve.wait_ge(stats_ready, n + 1)
                nc.vector.bn_aggr(mv[:, s], stats[:, s]).then_inc(mv_ready, 1)

            def middle(i, s):
                n = 2 * i + s
                dve.wait_ge(std_ready, n + 1)
                nc.vector.reciprocal(rstd[:, s], std[:, s]).then_inc(rstd_ready, 1)
                dve.wait_ge(rstd_ready, n + 1)
                nc.vector.scalar_tensor_tensor(out=nmean[:, s], in0=mv[:, s, 0:1], scalar=-1.0,
                                               in1=rstd[:, s], op0=ALU.mult,
                                               op1=ALU.mult).then_inc(nmean_ready, 1)

            def tail(i, s, first):
                n = 2 * i + s
                dve.wait_ge(yn_ready, n + 1)
                if not first:
                    dve.wait_ge(yo_ready, n - 1)
                nc.vector.tensor_tensor(yg[:, s], yn[:, s], g_sb[:, :], ALU.mult).then_inc(yg_ready, 1)

            def pair(i, first):
                head(i, 0, first)
                head(i, 1, first)
                middle(i, 0)
                middle(i, 1)
                tail(i, 0, first)
                tail(i, 1, first)

            pair(0, True)
            with dve.Fori(1, NT // 2) as i:
                pair(i, False)

        @block.scalar
        def _(act):
            act.wait_ge(eps_set, 1)

            def root(i, s):
                act.wait_ge(mv_ready, 2 * i + s + 1)
                nc.scalar.activation(std[:, s], mv[:, s, 1:2], ACT.Sqrt,
                                     bias=eps[:, :]).then_inc(std_ready, 1)

            def scale(i, s, first):
                n = 2 * i + s
                act.wait_ge(nmean_ready, n + 1)
                if not first:
                    act.wait_ge(yg_ready, n - 1)
                nc.scalar.activation(yn[:, s], y[:, s], ACT.Identity, bias=nmean[:, s],
                                     scale=rstd[:, s]).then_inc(yn_ready, 1)

            def store(i, s):
                act.wait_ge(yo_ready, 2 * i + s + 1)
                act.dma_start(out[bass.ds(i * (2 * P) + s * P, P)], yo[:, s]).then_inc(out_stored[s], 16)

            def pair(i, first):
                root(i, 0)
                root(i, 1)
                scale(i, 0, first)
                scale(i, 1, first)
                store(i, 0)
                store(i, 1)

            pair(0, True)
            with act.Fori(1, NT // 2) as i:
                pair(i, False)
            for s in range(2):
                act.wait_ge(out_stored[s], 16 * (NT // 2))


def kernel(x, ctx_4096, mask_BxS2_ik0, L0_xattn_Wq, L0_xattn_bq, L0_xattn_Wk, L0_xattn_bk,
           L0_xattn_Wv, L0_xattn_bv, L0_xattn_Wo, L0_xattn_bo, L0_xattn_ln_g, L0_xattn_ln_b):
    import numpy as np
    import concourse.bacc as bacc
    from concourse.bass_utils import run_bass_kernel_spmd

    def c(a):
        return np.ascontiguousarray(a)

    def weight(w):
        return c(np.asarray(w).T.reshape(KT, P, D).transpose(1, 0, 2).reshape(P, KT * D))

    def column(v):
        return c(np.asarray(v).reshape(KT, P).T)

    x = np.asarray(x)
    context = np.asarray(ctx_4096)
    rows = np.arange(P)
    head_mask = ((rows[:, None] % 64) // HD == np.arange(4)[None, :]).astype(np.float32)
    den_sel = ((rows[:, None] % 32 == HD) & (rows[:, None] // 32 == rows[None, :] // 32)).astype(np.float32)
    bv = np.asarray(L0_xattn_bv)
    bv_col = np.zeros((4, 32, NG * 2), bv.dtype)
    bv_col[:, 0:HD] = bv.reshape(NG * 2, 4, HD).transpose(1, 2, 0)

    arrays = {
        "ctxT": c(context.reshape(B, NP, SP_, KT, P).transpose(0, 1, 4, 3, 2)),
        "maskT": c(np.asarray(mask_BxS2_ik0).reshape(B, NC_, SC).transpose(0, 2, 1)),
        "xT": c(x.reshape(NQB, BPB * L, KT, P).transpose(0, 3, 2, 1)),
        "x_rows": c(x.reshape(ROWS, D)),
        "wqT": weight(L0_xattn_Wq), "wkT": weight(L0_xattn_Wk), "wvT": weight(L0_xattn_Wv),
        "woT": weight(L0_xattn_Wo),
        "bq": column(L0_xattn_bq), "bk": column(L0_xattn_bk), "bv_col": c(bv_col.reshape(P, NG * 2)),
        "bo": c(L0_xattn_bo), "ln_g": c(L0_xattn_ln_g), "ln_b": c(L0_xattn_ln_b),
        "ident": np.eye(P, dtype=np.float32), "head_mask": head_mask, "den_sel": den_sel,
    }
    nc = bacc.Bacc("TRN2", target_bir_lowering=False, num_devices=1)
    ap = {n: nc.dram_tensor(n, a.shape, mybir.dt.from_np(a.dtype), kind="ExternalInput").ap()
          for n, a in arrays.items()}
    q_scratch = nc.dram_tensor("q_scratch", (B, 64, NG, 2, L), F32, kind="Internal").ap()
    att_scratch = nc.dram_tensor("att_scratch", (NG * 2, 4, HD, B, L), F32, kind="Internal").ap()
    out = nc.dram_tensor("out", (ROWS, D), F32, kind="ExternalOutput").ap()
    build_attention(nc, ap["ctxT"], ap["maskT"], ap["xT"], ap["x_rows"], ap["wqT"], ap["wkT"],
                    ap["wvT"], ap["woT"], ap["bq"], ap["bk"], ap["bv_col"], ap["bo"], ap["ln_g"],
                    ap["ln_b"], ap["ident"], ap["head_mask"], ap["den_sel"], q_scratch,
                    att_scratch, out)
    build_output(nc, ap["x_rows"], ap["woT"], ap["bo"], ap["ln_g"], ap["ln_b"], att_scratch, out)
    r = run_bass_kernel_spmd(nc, [arrays], core_ids=[0])
    return r.results[0]["out"].reshape(B, L, D)
```

```python
from contextlib import ExitStack

import concourse.bass as bass
from concourse import mybir

F32 = mybir.dt.float32
F32R = mybir.dt.float32r
I32 = mybir.dt.int32
ALU = mybir.AluOpType
ACT = mybir.ActivationFunctionType
AX = mybir.AxisListType

P = 128
B, L, S, D = 32, 56, 1500, 512
NH, HD = 32, 16
KT = D // P
NG = 4
HG = NH // NG
SC = 125
NC_ = S // SC
NP = 6
SP_ = S // NP
NQ = 3
SQ = S // NQ
CQ = NC_ // NQ
NR = 3
NV = 3
DH = D // 2
HW = HG * L
HALF = HW // 2
PW = 2 * L
NQB = 4
BPB = B // NQB
ROWS = B * L
NT = ROWS // P
EPS = 1e-5
MASKED = -3.0e38
FLOOR = -1.0e38
MQ = HW // 4


def build_program(nc, ctxT, maskT, xT, x_rows, wqT, wkT, wvT, woT, bq, bk, bv, bo, ln_g,
                  ln_b, ident_in, head_mask_in, q_scratch, att_scratch, out):
    with ExitStack() as ctx:
        def sb(name, shape, dt=F32):
            return ctx.enter_context(nc.sbuf_tensor(name + "_sb", shape, dt))

        def psum(name, shape):
            return ctx.enter_context(nc.psum_tensor(name, shape, F32))

        def sem(name):
            return ctx.enter_context(nc.semaphore(name))

        s_buf = sb("s_buf", [P, 2, NC_, HW])
        k_a = sb("k_a", [P, S], F32R)
        k_b = sb("k_b", [P, S], F32R)
        v_sb = sb("v_sb", [P, NC_, D])
        qd_hi = sb("qd_hi", [P, 2, 2, HALF], F32R)
        qd_lo = sb("qd_lo", [P, 2, 2, HALF], F32R)
        q_raw = sb("q_raw", [P, NG, 2, L])
        q_hi = sb("q_hi", [P, NG, 2, L], F32R)
        q_lo = sb("q_lo", [P, NG, 2, L])
        mx = sb("mx", [P, 2, HW])
        mx_one = sb("mx_one", [P, HW])
        col_max = sb("col_max", [MQ, 4])
        diag_hi = sb("diag_hi", [MQ, 4, MQ], F32R)
        diag_lo = sb("diag_lo", [MQ, 4, MQ], F32R)
        col_hi = sb("col_hi", [MQ, 4], F32R)
        col_lo = sb("col_lo", [MQ, 4])
        mask_i = sb("mask_i", [P, NC_], I32)
        mask_bias = sb("mask_bias", [P, NC_])
        p_two = sb("p_two", [P, 2, HW])
        p_sum = sb("p_sum", [P, HW])
        o_rec = sb("o_rec", [P, PW])
        o_mul = sb("o_mul", [P, PW])
        o_out = sb("o_out", [P, NG, PW])
        ident = sb("ident", [P, P])
        ones = sb("ones", [P, P], F32R)
        head_mask = sb("head_mask", [P, 4])
        bq_sb = sb("bq_sb", [P, KT])
        bq_scaled = sb("bq_scaled", [P, KT])
        bk_sb = sb("bk_sb", [P, KT])
        bv_sb = sb("bv_sb", [P, NG])

        with ExitStack() as projections:
            def sb_proj(name, shape, dt=F32):
                return projections.enter_context(nc.sbuf_tensor(name + "_sb", shape, dt))

            raw = sb_proj("raw", [P, NR, KT, SP_])
            c_hi = sb_proj("c_hi", [P, KT, S], F32R)
            c_lo = sb_proj("c_lo", [P, KT, S], F32R)
            wk_hi = sb_proj("wk_hi", [P, KT, D], F32R)
            wk_lo = sb_proj("wk_lo", [P, KT, D], F32R)
            wv_hi = sb_proj("wv_hi", [P, KT, D], F32R)
            wv_lo = sb_proj("wv_lo", [P, KT, D], F32R)
        wo_out = sb("wo_out", [P, KT, D])
        bo_out = sb("bo_out", [P, D])
        assert 4 * (KT + 1) * D <= 4 * NR * KT * SP_
        att = sb("att", [P, KT, ROWS])
        y = sb("y", [P, NT, D])
        g_out = sb("g_out", [P, D])
        b_out = sb("b_out", [P, D])
        eps = sb("eps", [P, 1])
        stats = sb("stats", [P, 6])
        mv = sb("mv", [P, 2, 2])
        std = sb("std", [P, 2])
        rstd = sb("rstd", [P, 2])
        nmean = sb("nmean", [P, 2])

        stage = s_buf[:, :, :, :].rearrange("p a c n -> p (a c n)")
        wk_raw = stage[:, 0:KT * D]
        wv_raw = stage[:, KT * D:2 * KT * D]
        wq_raw = stage[:, 2 * KT * D:3 * KT * D].rearrange("p (k n) -> p k n", k=KT)
        NX = BPB * L
        x_at = 3 * KT * D
        x_raw = stage[:, x_at:x_at + 2 * KT * NX].rearrange("p (s k n) -> p s k n", s=2, k=KT)
        q_stage = v_sb[:, :, :].rearrange("p c n -> p (c n)")[:, 0:4 * NX].rearrange(
            "p (s n) -> p s n", s=4)

        ps_k = psum("ps_k", [P, 512])
        ps_v = psum("ps_v", [P, 512])
        ps_score = [psum(f"ps_score{i}", [P, 512]) for i in range(4)]
        ps_o = psum("ps_o", [P, 512])
        ps_max = psum("ps_max", [P, 512])

        weights_loaded = sem("weights_loaded")
        first_loaded = [sem(f"first_loaded{k}") for k in range(KT)]
        consts_loaded = sem("consts_loaded")
        x_loaded = [sem(f"x_loaded{i}") for i in range(2)]
        weights_split_hi = sem("weights_split_hi")
        weights_split_lo = sem("weights_split_lo")
        ones_set = sem("ones_set")
        bq_ready = sem("bq_ready")
        qproj_done = sem("qproj_done")
        q_evicted = sem("q_evicted")
        q_stored = [sem(f"q_stored{i}") for i in range(4)]
        raw_loaded = [sem(f"raw_loaded{i}") for i in range(NR)]
        batch_loaded = sem("batch_loaded")
        c_hi_ready = sem("c_hi_ready")
        c_lo_ready = sem("c_lo_ready")
        q_hi_ready = sem("q_hi_ready")
        q_lo_ready = sem("q_lo_ready")
        qd_ready = sem("qd_ready")
        mask_ready = sem("mask_ready")
        kproj_done = sem("kproj_done")
        k_hi_ready = sem("k_hi_ready")
        k_lo_ready = sem("k_lo_ready")
        vproj_done = sem("vproj_done")
        v_ready = sem("v_ready")
        scores_done = sem("scores_done")
        s_ready = sem("s_ready")
        s_ready_v = sem("s_ready_v")
        max_step = sem("max_step")
        maxT_done = sem("maxT_done")
        colmax_ready = sem("colmax_ready")
        colhi_ready = sem("colhi_ready")
        collo_ready = sem("collo_ready")
        diag_ready = sem("diag_ready")
        spread_done = sem("spread_done")
        shifted = sem("shifted")
        exp_done = sem("exp_done")
        pv_done = sem("pv_done")
        sum_step = sem("sum_step")
        rec_ready = sem("rec_ready")
        mul_ready = sem("mul_ready")
        o_ready = sem("o_ready")
        att_stored = sem("att_stored")
        wo_loaded = sem("wo_loaded")
        ln_loaded = sem("ln_loaded")
        att_loaded = [sem(f"att_loaded{i}") for i in range(3)]
        x_in = [sem(f"x_in{i}") for i in range(2)]
        eps_set = sem("eps_set")
        xb_ready = sem("xb_ready")
        out_done = sem("out_done")
        y_ready = sem("y_ready")
        stats_ready = sem("stats_ready")
        mv_ready = sem("mv_ready")
        std_ready = sem("std_ready")
        rstd_ready = sem("rstd_ready")
        nmean_ready = sem("nmean_ready")
        yn_ready = sem("yn_ready")
        yg_ready = sem("yg_ready")
        yo_ready = sem("yo_ready")
        out_stored = sem("out_stored")

        SPLIT_AT = (6, 7, 8, 11, 12, 13)
        NMAX = 6
        NSUM = 6
        SH = 4
        NSH = NC_ // SH
        BATCH_DMA = 48

        NT_ATT = (0, 4, NT - 1, NT)
        assert (NT - 1) * P <= (B - 1) * L
        NB = 6
        SV = (1, 4)
        NSA = NC_ - len(SV)

        def evicted(t, c):
            return t * NSA + sum(i not in SV for i in range(c + 1))

        block = ctx.enter_context(nc.Block())

        @block.sync
        def _(sp):
            for k in range(KT):
                sp.dma_start(wq_raw[:, k], wqT.rearrange("p (k n) -> p k n", k=KT)[:, k]).then_inc(
                    first_loaded[k], 16)
                sp.dma_start(x_raw[:, 0, k], xT[0][:, k]).then_inc(first_loaded[k], 16)
            for dst, src in ((ident[:, :], ident_in), (head_mask[:, :], head_mask_in),
                             (bq_sb[:, :], bq), (bk_sb[:, :], bk), (bv_sb[:, :], bv)):
                sp.dma_start(dst, src).then_inc(consts_loaded, 16)
            sp.dma_start(x_raw[:, 1], xT[1]).then_inc(x_loaded[1], 16)
            sp.dma_start(wk_raw, wkT).then_inc(weights_loaded, 16)
            sp.dma_start(wv_raw, wvT).then_inc(weights_loaded, 16)

            def load_piece(b, i, first):
                if not (first and i < NR):
                    sp.wait_ge(c_hi_ready, b * NP + (i + 1 - NR))
                    sp.wait_ge(c_lo_ready, b * NP + (i + 1 - NR))
                sp.dma_start(raw[:, i % NR], ctxT[bass.ds(b, 1), i].rearrange(
                    "o p k n -> (o p) k n")).then_inc(raw_loaded[i % NR], 16)

            def load_queries(b, first):
                if not first:
                    sp.wait_ge(q_lo_ready, b)
                    sp.wait_ge(mask_ready, b)
                for half in range(2):
                    sp.dma_start(q_raw[64 * half:64 * half + 64], q_scratch[bass.ds(b, 1)].rearrange(
                        "o p g s l -> (o p) g s l")).then_inc(batch_loaded, 16)
                sp.dma_start(mask_i[0:SC, :], maskT[bass.ds(b, 1)].rearrange(
                    "o p c -> (o p) c")).then_inc(batch_loaded, 16)

            def store_attention(b):
                sp.wait_ge(o_ready, (b + 1) * NG)
                for j in range(4):
                    for e in range(2):
                        rows = slice(32 * j + HD * e, 32 * j + HD * (e + 1))
                        sp.dma_start(att_scratch[:, j, e, :, bass.ds(b, 1)].rearrange(
                            "g d o l -> d g (o l)"),
                            o_out[rows, :, e * L:(e + 1) * L]).then_inc(att_stored, 16)

            for i in range(NR):
                load_piece(0, i, True)
            for n in range(NQB):
                for g in range(NG):
                    i = n * NG + g
                    sp.wait_ge(q_evicted, i + 1)
                    for s in range(2):
                        sp.dma_start(
                            q_scratch[n * BPB:(n + 1) * BPB, :, g, s].rearrange("b p l -> p b l"),
                            q_stage[64 * s:64 * s + 64, i % 4].rearrange("p (b l) -> p b l", b=BPB),
                        ).then_inc(q_stored[i % 4], 16)
                    if n == 2 and g < NP - NR:
                        load_piece(0, NR + g, True)
                if n + 2 < NQB:
                    sp.wait_ge(qproj_done, (n + 1) * NG)
                    sp.dma_start(x_raw[:, n % 2], xT[n + 2]).then_inc(x_loaded[n % 2], 16)
                if n == 0:
                    for i in range(4):
                        sp.wait_ge(q_stored[i], 32)
                    load_queries(0, True)
            for i in range(4):
                sp.wait_ge(q_stored[i], 32 * NQB)
            for i in range(NP):
                if i == NR:
                    load_queries(1, False)
                load_piece(1, i, False)
            with sp.Fori(1, B - 1) as b:
                store_attention(b - 1)
                for i in range(NP):
                    if i == NR:
                        load_queries(b + 1, False)
                    load_piece(b + 1, i, False)
            store_attention(B - 2)
            sp.wait_ge(c_hi_ready, B * NP)
            sp.wait_ge(c_lo_ready, B * NP)
            sp.dma_start(wo_out[:, :, :], woT.rearrange("p (k n) -> p k n", k=KT)).then_inc(wo_loaded, 16)
            sp.dma_start(bo_out[:, :], bo.partition_broadcast(P)).then_inc(wo_loaded, 16)

            def load_att(i):
                rows = slice(NT_ATT[i] * P, NT_ATT[i + 1] * P)
                sp.dma_start(att[:, :, rows], att_scratch.rearrange(
                    "g j e d b l -> (j e d) g (b l)")[:, :, rows]).then_inc(att_loaded[i], 16)

            def load_x(i):
                tiles = slice(i * (NT // 2), (i + 1) * (NT // 2))
                sp.dma_start(y[:, tiles], x_rows.rearrange("(i p) n -> p i n", p=P)[:, tiles]).then_inc(
                    x_in[i], 16)

            sp.wait_ge(kproj_done, B * NG * NQ)
            sp.wait_ge(vproj_done, B * NG * NV)
            sp.wait_ge(att_stored, 128 * (B - 1))
            load_att(0)
            load_x(0)
            sp.dma_start(g_out[:, :], ln_g.partition_broadcast(P)).then_inc(ln_loaded, 16)
            sp.dma_start(b_out[:, :], ln_b.partition_broadcast(P)).then_inc(ln_loaded, 16)
            load_att(1)
            load_x(1)
            store_attention(B - 1)
            sp.wait_ge(att_stored, 128 * B)
            load_att(2)

            def store_tiles(n, count):
                sp.wait_ge(yo_ready, n + count)
                sp.dma_start(out[bass.ds(n * P, count * P)].rearrange("(i p) n -> p i n", p=P),
                             y[:, bass.ds(n, count)]).then_inc(out_stored, 16)

            with sp.Fori(0, NT // 2 - 1) as i:
                store_tiles(i * 2, 2)
            store_tiles(NT - 2, 1)
            store_tiles(NT - 1, 1)
            sp.wait_ge(out_stored, 16 * (NT // 2 + 1))

        @block.tensor
        def _(pe):
            for k in range(KT):
                pe.wait_ge(first_loaded[k], 32)
                for g in range(NG):
                    mm = nc.tensor.matmul(ps_score[g][:, 0:NX], wq_raw[:, k, g * P:(g + 1) * P],
                                          x_raw[:, 0, k], start=(k == 0), stop=(k == KT - 1))
                    if k == KT - 1:
                        mm.then_inc(qproj_done, 1)
            for n in range(1, NQB):
                pe.wait_ge(x_loaded[n % 2], 16 * ((n + 1) // 2))
                for g in range(NG):
                    i = n * NG + g
                    pe.wait_ge(q_evicted, i - 3)
                    for k in range(KT):
                        mm = nc.tensor.matmul(ps_score[i % 4][:, 0:NX], wq_raw[:, k, g * P:(g + 1) * P],
                                              x_raw[:, n % 2, k], start=(k == 0), stop=(k == KT - 1))
                    mm.then_inc(qproj_done, 1)
            pe.wait_ge(consts_loaded, 80)
            pe.wait_ge(ones_set, 1)
            pe.wait_ge(weights_split_hi, 2)
            pe.wait_ge(weights_split_lo, 2)

            def project_k(t, b, g, q, first, between=None):
                if g == 0:
                    pe.wait_ge(c_hi_ready, b * NP + 2 * q + 2)
                    pe.wait_ge(c_lo_ready, b * NP + 2 * q + 2)
                if not (first and g == 0 and q == 0):
                    pe.wait_ge(k_lo_ready, t * NQ + q)
                bank = ps_k[:, 0:SQ]
                keys = slice(q * SQ, (q + 1) * SQ)
                cols = slice(g * P, (g + 1) * P)
                for k in range(KT):
                    if k == 2 and between is not None:
                        max_transposes(between)
                    nc.tensor.matmul(bank, wk_hi[:, k, cols], c_hi[:, k, keys], start=(k == 0), stop=False)
                    nc.tensor.matmul(bank, wk_hi[:, k, cols], c_lo[:, k, keys], start=False, stop=False)
                    mm = nc.tensor.matmul(bank, wk_lo[:, k, cols], c_hi[:, k, keys], start=False,
                                          stop=(k == KT - 1))
                mm.then_inc(kproj_done, 1)

            def project_v(t, g, n, first):
                if not (first and g == 0 and n == 0):
                    pe.wait_ge(v_ready, t * NV + n)
                half = slice((g // 2) * DH, (g // 2 + 1) * DH)
                for c in range(2):
                    at = ((g % 2) * 2 * NV + 2 * n + c) * SC
                    keys = slice(at, at + SC)
                    bank = ps_v[0:SC, c * DH:(c + 1) * DH]
                    for k in range(KT):
                        hi, lo = c_hi[:, k, keys], c_lo[:, k, keys]
                        nc.tensor.matmul(bank, hi, wv_hi[:, k, half], start=(k == 0), stop=False)
                        nc.tensor.matmul(bank, hi, wv_lo[:, k, half], start=False, stop=False)
                        mm = nc.tensor.matmul(bank, lo, wv_hi[:, k, half], start=False,
                                              stop=(k == KT - 1))
                mm.then_inc(vproj_done, 1)

            def scores(t, g, first):
                pe.wait_ge(qd_ready, t + 1)
                for c in range(NC_):
                    if c % CQ == 0:
                        pe.wait_ge(k_hi_ready, 2 * (t * NQ + c // CQ + 1))
                        pe.wait_ge(k_lo_ready, t * NQ + c // CQ + 1)
                    if not (first and g == 0 and c < 4):
                        if (c - 4) % NC_ in SV:
                            pe.wait_ge(s_ready_v, (t if c >= 4 else t - 1) * len(SV)
                                       + SV.index((c - 4) % NC_) + 1)
                        else:
                            pe.wait_ge(s_ready, evicted(t, c - 4) if c >= 4
                                       else evicted(t - 1, c - 4 + NC_))
                    bank = ps_score[c % 4]
                    for s, kk in enumerate((k_a, k_b)):
                        w = kk[:, c * SC:(c + 1) * SC]
                        o = bank[0:SC, s * HALF:(s + 1) * HALF]
                        nc.tensor.matmul(o, w, qd_hi[:, g % 2, s], start=True, stop=False)
                        mm = nc.tensor.matmul(o, w, qd_lo[:, g % 2, s], start=False, stop=True)
                    mm.then_inc(scores_done, 1)

            def max_transposes(t):
                pe.wait_ge(max_step, (t + 1) * NMAX)
                if not (isinstance(t, int) and t == 0):
                    pe.wait_ge(shifted, t * NSH)
                for i in range(4):
                    mm = nc.tensor.transpose(ps_max[0:MQ, i * SC:(i + 1) * SC],
                                             mx_one[0:SC, i * MQ:(i + 1) * MQ], ident[0:SC, 0:SC])
                mm.then_inc(maxT_done, 1)

            def max_spread(t):
                pe.wait_ge(diag_ready, t + 1)
                top = ps_max[0:SC, 0:HW]
                nc.tensor.matmul(top, ones[0:MQ, 0:SC], diag_hi[:, :, :].rearrange("p a n -> p (a n)"),
                                 start=True, stop=False)
                nc.tensor.matmul(top, ones[0:MQ, 0:SC], diag_lo[:, :, :].rearrange("p a n -> p (a n)"),
                                 start=False, stop=True).then_inc(spread_done, 1)

            def times_v(t, g):
                if not (isinstance(t, int) and t == 0):
                    pe.wait_ge(mul_ready, t)
                if g % 2 == 0:
                    pe.wait_ge(v_ready, (t + 2) * NV)
                for c in range(NC_):
                    if c % SH == 0:
                        pe.wait_ge(exp_done, t * NSH + c // SH + 1)
                    for j in range(4):
                        at = g * P + 32 * j
                        nc.tensor.matmul(
                            ps_o[32 * j:32 * j + 32, 0:PW], v_sb[0:SC, c, at:at + 32],
                            s_buf[0:SC, g % 2, c, j * PW:(j + 1) * PW],
                            start=(c == 0), stop=(c == NC_ - 1), skip_group_check=True)

            def denominators(t):
                pe.wait_ge(sum_step, (t + 1) * NSUM)
                for j in range(4):
                    mm = nc.tensor.matmul(
                        ps_o[32 * j:32 * j + 32, PW:2 * PW], ones[0:SC, 0:32].bitcast(F32),
                        p_sum[0:SC, j * PW:(j + 1) * PW], start=True, stop=True, skip_group_check=True)
                mm.then_inc(pv_done, 1)

            def step(b, g, first):
                t = b * NG + g
                begun = not (first and g == 0)
                ended = not (first and g < 2)
                project_k(t, b, g, 0, first)
                project_v(t, g, 0, first)
                project_k(t, b, g, 1, first, between=t - 1 if begun else None)
                project_v(t, g, 1, first)
                if begun:
                    max_spread(t - 1)
                project_k(t, b, g, 2, first)
                project_v(t, g, 2, first)
                if ended:
                    times_v(t - 2, (g - 2) % NG)
                    denominators(t - 2)
                scores(t, g, first)

            for g in range(NG):
                step(0, g, True)
            with pe.Fori(1, B) as b:
                for g in range(NG):
                    step(b, g, False)

            def out_tile(n, bank):
                for k in range(KT):
                    mm = nc.tensor.matmul(bank[:, :], att[:, k, n * P:(n + 1) * P], wo_out[:, k],
                                          start=(k == 0), stop=(k == KT - 1))
                mm.then_inc(out_done, 1)

            banks = [ps_k, ps_v] + ps_score
            last = B * NG - 1
            pe.wait_ge(wo_loaded, 32)
            pe.wait_ge(att_loaded[0], 16)
            pe.wait_ge(k_lo_ready, B * NG * NQ)
            out_tile(0, banks[0])
            pe.wait_ge(v_ready, B * NG * NV)
            out_tile(1, banks[1])
            max_transposes(last)
            times_v(last - 1, NG - 2)
            denominators(last - 1)
            max_spread(last)
            pe.wait_ge(s_ready, B * NG * NSA)
            out_tile(2, banks[2])
            out_tile(3, banks[3])
            times_v(last, NG - 1)
            pe.wait_ge(att_loaded[1], 16)
            out_tile(4, banks[4])
            out_tile(5, banks[5])
            denominators(last)
            pe.wait_ge(y_ready, 1)
            out_tile(6, banks[0])
            pe.wait_ge(y_ready, 2)
            out_tile(7, banks[1])
            for n in range(NB + 2, NT - 2):
                pe.wait_ge(y_ready, n - 1)
                out_tile(n, banks[n % 2])
            pe.wait_ge(y_ready, NT - 3)
            out_tile(NT - 2, banks[0])
            pe.wait_ge(att_loaded[2], 16)
            pe.wait_ge(y_ready, NT - 2)
            out_tile(NT - 1, banks[1])

        @block.scalar
        def _(act):
            def split_hi(b, i, first):
                act.wait_ge(raw_loaded[i % NR], (b * 2 + i // NR + 1) * 16)
                if not first:
                    act.wait_ge(kproj_done, (b * NG - 1) * NQ + i // 2 + 1)
                    if i >= NV:
                        act.wait_ge(vproj_done, (b * NG - 1) * NV + i - NV + 1)
                nc.scalar.copy(c_hi[:, :, i * SP_:(i + 1) * SP_], raw[:, i % NR]).then_inc(c_hi_ready, 1)

            act.wait_ge(consts_loaded, 80)
            nc.scalar.mul(bq_scaled[:, :], bq_sb[:, :], HD ** -0.5).then_inc(bq_ready, 1)
            act.wait_ge(bq_ready, 1)
            for i in range(NQB * NG):
                if i == 4:
                    act.wait_ge(weights_loaded, 32)
                    nc.scalar.copy(wk_hi[:, :, :].rearrange("p k n -> p (k n)"), wk_raw).then_inc(weights_split_hi, 1)
                if i == 5:
                    nc.scalar.copy(wv_hi[:, :, :].rearrange("p k n -> p (k n)"), wv_raw).then_inc(weights_split_hi, 1)
                if i in SPLIT_AT:
                    split_hi(0, SPLIT_AT.index(i), True)
                act.wait_ge(qproj_done, i + 1)
                if i >= 4:
                    act.wait_ge(q_stored[i % 4], 32 * (i // 4))
                nc.scalar.activation(q_stage[:, i % 4], ps_score[i % 4][:, 0:NX], ACT.Identity,
                                     bias=bq_scaled[:, i % NG:i % NG + 1],
                                     scale=HD ** -0.5).then_inc(q_evicted, 1)
            def round_queries(b):
                act.wait_ge(batch_loaded, (b + 1) * BATCH_DMA)
                if not (isinstance(b, int) and b == 0):
                    act.wait_ge(qd_ready, b * NG)
                nc.scalar.copy(q_hi[:, :, :, :], q_raw[:, :, :, :]).then_inc(q_hi_ready, 1)

            def evict_k_hi(t, g, q, first):
                act.wait_ge(kproj_done, t * NQ + q + 1)
                if not (first and g == 0) and q == 0:
                    act.wait_ge(scores_done, t * NC_)
                cols = slice(q * SQ, (q + 1) * SQ)
                bank = ps_k
                nc.scalar.activation(k_a[0:64, cols], bank[0:64, 0:SQ], ACT.Identity,
                                     bias=bk_sb[0:64, g:g + 1]).then_inc(k_hi_ready, 1)
                nc.scalar.activation(k_b[64:128, cols], bank[64:128, 0:SQ], ACT.Identity,
                                     bias=bk_sb[64:128, g:g + 1]).then_inc(k_hi_ready, 1)

            def exps(t, g, i):
                act.wait_ge(shifted, t * NSH + i + 1)
                part = s_buf[0:SC, g % 2, i * SH:(i + 1) * SH]
                nc.scalar.activation(part, part, ACT.Exp).then_inc(exp_done, 1)

            def evict_v(t, g, n, first):
                act.wait_ge(vproj_done, t * NV + n + 1)
                if not first and g % 2 == 0 and n == 0:
                    act.wait_ge(pv_done, t - 2)
                c = (g % 2) * 2 * NV + 2 * n
                half = slice((g // 2) * DH, (g // 2 + 1) * DH)
                nc.scalar.copy(v_sb[0:SC, c:c + 2, half], ps_v[0:SC, :].rearrange(
                    "p (c n) -> p c n", c=2)).then_inc(v_ready, 1)

            def evict_scores(t, b, g, first):
                if g == 0:
                    act.wait_ge(mask_ready, b + 1)
                if not (first and g < 2):
                    act.wait_ge(pv_done, t - 1)
                for c in (c for c in range(NC_) if c not in SV):
                    act.wait_ge(scores_done, t * NC_ + c + 1)
                    nc.scalar.activation(s_buf[0:SC, g % 2, c], ps_score[c % 4][0:SC, 0:HW],
                                         ACT.Identity, bias=mask_bias[0:SC, c:c + 1]).then_inc(s_ready, 1)

            round_queries(0)

            def step(b, g, first, last):
                t = b * NG + g
                begun = not (first and g == 0)
                if g == 0 and not first:
                    split_hi(b, 4, False)
                    split_hi(b, 5, False)
                evict_k_hi(t, g, 0, first)
                if first and g == 0:
                    for i in range(4):
                        act.wait_ge(q_stored[i], 32 * NQB)
                evict_v(t, g, 0, first)
                if g == 3 and not last:
                    round_queries(b + 1)
                    split_hi(b + 1, 0, False)
                    split_hi(b + 1, 1, False)
                evict_k_hi(t, g, 1, first)
                evict_v(t, g, 1, first)
                if g == 3 and not last:
                    split_hi(b + 1, 2, False)
                if begun:
                    exps(t - 1, (g - 1) % NG, 0)
                evict_k_hi(t, g, 2, first)
                if g == 3 and not last:
                    split_hi(b + 1, 3, False)
                if begun:
                    exps(t - 1, (g - 1) % NG, 1)
                evict_v(t, g, 2, first)
                if begun:
                    exps(t - 1, (g - 1) % NG, 2)
                evict_scores(t, b, g, first)

            act.wait_ge(weights_split_lo, 2)
            for g in range(NG):
                step(0, g, True, False)
            with act.Fori(1, B - 1) as b:
                for g in range(NG):
                    step(b, g, False, False)
            for g in range(NG):
                step(B - 1, g, False, True)
            for i in range(NSH):
                exps(B * NG - 1, NG - 1, i)

            def root(n, s):
                act.wait_ge(mv_ready, n + 1)
                nc.scalar.activation(std[:, s:s + 1], mv[:, s, 1:2], ACT.Sqrt,
                                     bias=eps[:, :]).then_inc(std_ready, 1)

            def scale(n, s):
                act.wait_ge(nmean_ready, n + 1)
                row = y[:, bass.ds(n, 1)].rearrange("p a n -> p (a n)")
                nc.scalar.activation(row, row, ACT.Identity, bias=nmean[:, s:s + 1],
                                     scale=rstd[:, s:s + 1]).then_inc(yn_ready, 1)

            act.wait_ge(eps_set, 1)
            root(0, 0)
            with act.Fori(0, NT // 2 - 1) as i:
                root(i * 2 + 1, 1)
                scale(i * 2, 0)
                root(i * 2 + 2, 0)
                scale(i * 2 + 1, 1)
            root(NT - 1, 1)
            scale(NT - 2, 0)
            scale(NT - 1, 1)

        @block.vector
        def _(dve):
            nc.vector.memset(ones[:, :].bitcast(F32), 1.0).then_inc(ones_set, 1)
            for hi, lo, w, n in ((wk_hi, wk_lo, wk_raw, 1), (wv_hi, wv_lo, wv_raw, 2)):
                dve.wait_ge(weights_split_hi, n)
                nc.vector.tensor_tensor(lo[:, :, :].rearrange("p k n -> p (k n)"), w,
                                        hi[:, :, :].rearrange("p k n -> p (k n)").bitcast(F32),
                                        ALU.subtract).then_inc(weights_split_lo, 1)
            def evict_k_lo(t, g, q):
                dve.wait_ge(k_hi_ready, 2 * (t * NQ + q) + 1)
                cols = slice(q * SQ, (q + 1) * SQ)
                bank = ps_k
                nc.vector.scalar_tensor_tensor(
                    out=k_a[64:128, cols], in0=bank[0:64, 0:SQ], scalar=bk_sb[0:64, g:g + 1],
                    in1=k_a[0:64, cols].bitcast(F32), op0=ALU.add, op1=ALU.subtract)
                dve.wait_ge(k_hi_ready, 2 * (t * NQ + q) + 2)
                nc.vector.scalar_tensor_tensor(
                    out=k_b[0:64, cols], in0=bank[64:128, 0:SQ], scalar=bk_sb[64:128, g:g + 1],
                    in1=k_b[64:128, cols].bitcast(F32), op0=ALU.add, op1=ALU.subtract).then_inc(k_lo_ready, 1)

            def evict_scores(t, b, g):
                if not (isinstance(t, int) and t < 2):
                    dve.wait_ge(pv_done, t - 1)
                dve.wait_ge(mask_ready, b + 1)
                for c in SV:
                    dve.wait_ge(scores_done, t * NC_ + c + 1)
                    nc.vector.tensor_scalar(s_buf[0:SC, g % 2, c], ps_score[c % 4][0:SC, 0:HW],
                                            mask_bias[0:SC, c:c + 1], None, ALU.add).then_inc(s_ready_v, 1)

            def chunk_max(t, g, first):
                part = s_buf[0:SC, g % 2]
                acc = mx[0:SC]
                for i in range(5):
                    dve.wait_ge(s_ready, evicted(t, 2 * i + 3))
                    if i == 0:
                        dve.wait_ge(s_ready_v, (t + 1) * len(SV))
                    if i:
                        dve.wait_ge(max_step, t * NMAX + i)
                    nc.vector.tensor_tensor(acc, part[:, 2 * i + 2:2 * i + 4], acc if i else part[:, 0:2],
                                            ALU.max).then_inc(max_step, 1)

            def last_max(t):
                acc = mx[0:SC]
                if not (isinstance(t, int) and t == 0):
                    dve.wait_ge(maxT_done, t)
                dve.wait_ge(max_step, t * NMAX + 5)
                nc.vector.scalar_tensor_tensor(out=mx_one[0:SC], in0=acc[:, 0], scalar=FLOOR, in1=acc[:, 1],
                                               op0=ALU.max, op1=ALU.max).then_inc(max_step, 1)

            def mask_to_bias(b):
                dve.wait_ge(batch_loaded, (b + 1) * BATCH_DMA)
                if not (isinstance(b, int) and b == 0):
                    dve.wait_ge(s_ready, b * NG * NSA)
                nc.vector.tensor_scalar(mask_bias[0:SC, :], mask_i[0:SC, :], 0, MASKED, ALU.is_equal,
                                        ALU.mult).then_inc(mask_ready, 1)

            def partition_max(t):
                dve.wait_ge(maxT_done, t + 1)
                nc.vector.tensor_reduce(col_max[:, :], ps_max[0:MQ, 0:4 * SC].rearrange(
                    "p (a n) -> p a n", a=4), AX.X, ALU.max).then_inc(colmax_ready, 1)
                dve.wait_ge(colmax_ready, t + 1)
                nc.vector.tensor_copy(col_hi[:, :], col_max[:, :]).then_inc(colhi_ready, 1)
                for dst, src in ((diag_hi, col_hi[:, :].bitcast(F32)), (diag_lo, col_lo[:, :])):
                    if dst is diag_hi:
                        dve.wait_ge(colhi_ready, t + 1)
                        nc.vector.tensor_tensor(col_lo[:, :], col_max[:, :], src,
                                                ALU.subtract).then_inc(collo_ready, 1)
                    else:
                        dve.wait_ge(collo_ready, t + 1)
                    ins = nc.vector.tensor_tensor(
                        dst[:, :, :], ident[0:MQ, 0:MQ].unsqueeze(1).to_broadcast([MQ, 4, MQ]),
                        src.unsqueeze(2).to_broadcast([MQ, 4, MQ]), ALU.mult)
                ins.then_inc(diag_ready, 1)

            def shift(t, g):
                dve.wait_ge(spread_done, t + 1)
                top = ps_max[0:SC, 0:HW].unsqueeze(1).to_broadcast([SC, SH, HW])
                for i in range(NSH):
                    part = s_buf[0:SC, g % 2, i * SH:(i + 1) * SH]
                    nc.vector.tensor_tensor(part, part, top, ALU.subtract).then_inc(shifted, 1)

            def normalise(t, g, b):
                dve.wait_ge(pv_done, t + 1)
                nc.vector.reciprocal(o_rec[:, :], ps_o[:, PW:2 * PW]).then_inc(rec_ready, 1)
                dve.wait_ge(rec_ready, t + 1)
                nc.vector.tensor_tensor(o_mul[:, :], ps_o[:, 0:PW], o_rec[:, :], ALU.mult).then_inc(mul_ready, 1)
                dve.wait_ge(mul_ready, t + 1)
                if g == 0 and not (isinstance(b, int) and b == 0):
                    dve.wait_ge(att_stored, b * 128)
                nc.vector.tensor_tensor(
                    o_out[:, g], o_mul[:, :], bv_sb[:, g:g + 1].to_broadcast([P, PW]), ALU.add).then_inc(o_ready, 1)

            def step(b, g, first, last):
                t = b * NG + g
                begun = not (first and g == 0)
                evict_k_lo(t, g, 0)
                if begun:
                    last_max(t - 1)
                if not (first and g < 3):
                    normalise(t - 3, (g - 3) % NG, b if g == 3 else b - 1)
                if begun:
                    partition_max(t - 1)
                evict_k_lo(t, g, 1)
                if begun:
                    shift(t - 1, (g - 1) % NG)
                evict_k_lo(t, g, 2)
                evict_scores(t, b, g)
                chunk_max(t, g, first)
                if g == 3 and not last:
                    mask_to_bias(b + 1)

            mask_to_bias(0)
            for g in range(NG):
                step(0, g, True, False)
            with dve.Fori(1, B - 1) as b:
                for g in range(NG):
                    step(b, g, False, False)
            for g in range(NG):
                step(B - 1, g, False, True)
            last = B * NG - 1
            normalise(last - 2, NG - 3, B - 1)
            last_max(last)
            partition_max(last)
            shift(last, NG - 1)
            normalise(last - 1, NG - 2, B - 1)

            banks = [ps_k, ps_v] + ps_score

            def tile_sum(n, s, bank):
                row = y[:, bass.ds(n, 1)].rearrange("p a n -> p (a n)")
                dve.wait_ge(out_done, n + 1)
                dve.wait_ge(xb_ready, n + 1)
                nc.vector.tensor_tensor(row, bank[:, :], row, ALU.add).then_inc(y_ready, 1)
                dve.wait_ge(wo_loaded, 32)
                dve.wait_ge(y_ready, n + 1)
                nc.vector.bn_stats(stats[:, :], row).then_inc(stats_ready, 1)
                dve.wait_ge(wo_loaded, 32)
                dve.wait_ge(stats_ready, n + 1)
                nc.vector.bn_aggr(mv[:, s], stats[:, :]).then_inc(mv_ready, 1)

            def tile_scale(n, s):
                dve.wait_ge(std_ready, n + 1)
                nc.vector.reciprocal(rstd[:, s:s + 1], std[:, s:s + 1]).then_inc(rstd_ready, 1)
                dve.wait_ge(rstd_ready, n + 1)
                nc.vector.scalar_tensor_tensor(
                    out=nmean[:, s:s + 1], in0=mv[:, s, 0:1], scalar=-1.0, in1=rstd[:, s:s + 1],
                    op0=ALU.mult, op1=ALU.mult).then_inc(nmean_ready, 1)

            def tile_gain(n):
                row = y[:, bass.ds(n, 1)].rearrange("p a n -> p (a n)")
                dve.wait_ge(yn_ready, n + 1)
                nc.vector.tensor_tensor(row, row, g_out[:, :], ALU.mult).then_inc(yg_ready, 1)

            dve.wait_ge(vproj_done, B * NG * NV)
            nc.vector.memset(eps[:, :], EPS).then_inc(eps_set, 1)
            tile_sum(0, 0, banks[0])
            tile_sum(1, 1, banks[1])
            tile_scale(0, 0)
            tile_sum(2, 0, banks[2])
            tile_scale(1, 1)
            dve.wait_ge(ln_loaded, 32)
            for n in range(3, NB):
                tile_sum(n, n % 2, banks[n])
                tile_gain(n - 3)
                tile_scale(n - 1, (n - 1) % 2)
            normalise(last, NG - 1, B - 1)
            with dve.Fori(NB // 2, NT // 2) as i:
                for s in range(2):
                    n = i * 2 + s
                    tile_sum(n, s, banks[s])
                    tile_gain(n - 3)
                    tile_scale(n - 1, 1 - s)
            tile_gain(NT - 3)
            tile_scale(NT - 1, 1)
            tile_gain(NT - 2)
            tile_gain(NT - 1)

        @block.gpsimd
        def _(pool):
            def split_lo(b, i):
                pool.wait_ge(c_hi_ready, b * NP + i + 1)
                keys = slice(i * SP_, (i + 1) * SP_)
                nc.gpsimd.tensor_tensor(c_lo[:, :, keys], raw[:, i % NR], c_hi[:, :, keys].bitcast(F32),
                                        ALU.subtract).then_inc(c_lo_ready, 1)

            def split_queries(b):
                pool.wait_ge(q_hi_ready, b + 1)
                nc.gpsimd.tensor_tensor(q_lo[:, :, :, :], q_raw[:, :, :, :], q_hi[:, :, :, :].bitcast(F32),
                                        ALU.subtract).then_inc(q_lo_ready, 1)

            def sum_chunks(t, g):
                part = s_buf[0:SC, g % 2]
                acc = p_two[0:SC]
                for i in range(5):
                    pool.wait_ge(exp_done, t * NSH + (2 * i + 3) // SH + 1)
                    if i or not (isinstance(t, int) and t == 0):
                        pool.wait_ge(sum_step, t * NSUM + i)
                    nc.gpsimd.tensor_tensor(acc, part[:, 2 * i + 2:2 * i + 4], acc if i else part[:, 0:2],
                                            ALU.add).then_inc(sum_step, 1)
                if not (isinstance(t, int) and t == 0):
                    pool.wait_ge(pv_done, t)
                pool.wait_ge(sum_step, t * NSUM + 5)
                nc.gpsimd.tensor_tensor(p_sum[0:SC], acc[:, 0], acc[:, 1], ALU.add).then_inc(sum_step, 1)

            def query_blocks(t, b, g, first):
                if not (first and g < 2):
                    pool.wait_ge(scores_done, (t - 1) * NC_)
                pool.wait_ge(q_lo_ready, b + 1)
                for dst, src in ((qd_hi, q_hi), (qd_lo, q_lo)):
                    for s in range(2):
                        q = src[:, g, s] if src is q_lo else src[:, g, s].bitcast(F32)
                        last = nc.gpsimd.tensor_tensor(
                            dst[:, g % 2, s].rearrange("p (h l) -> p h l", h=4),
                            q.unsqueeze(1).to_broadcast([P, 4, L]),
                            head_mask[:, :].unsqueeze(2).to_broadcast([P, 4, L]), ALU.mult)
                last.then_inc(qd_ready, 1)

            pool.wait_ge(consts_loaded, 80)
            for i in range(NP):
                split_lo(0, i)
            split_queries(0)
            query_blocks(0, 0, 0, True)

            def step(b, g, first, last):
                t = b * NG + g
                if g == 0 and not first:
                    split_lo(b, 4)
                    split_lo(b, 5)
                if not (first and g < 2):
                    sum_chunks(t - 2, (g - 2) % NG)
                if g < 3:
                    query_blocks(t + 1, b, g + 1, first)
                elif not last:
                    split_queries(b + 1)
                    query_blocks(t + 1, b + 1, 0, False)
                    for i in range(4):
                        split_lo(b + 1, i)

            for g in range(NG):
                step(0, g, True, False)
            with pool.Fori(1, B - 1) as b:
                for g in range(NG):
                    step(b, g, False, False)
            for g in range(NG):
                step(B - 1, g, False, True)
            def add_bo(i):
                pair = y[:, bass.ds(i * 2, 2)]
                nc.gpsimd.tensor_tensor(pair, pair, bo_out[:, :].unsqueeze(1).to_broadcast([P, 2, D]),
                                        ALU.add).then_inc(xb_ready, 2)

            def add_ln_b(n):
                row = y[:, bass.ds(n, 1)].rearrange("p a n -> p (a n)")
                pool.wait_ge(yg_ready, n + 1)
                nc.gpsimd.tensor_tensor(row, row, b_out[:, :], ALU.add).then_inc(yo_ready, 1)

            sum_chunks(B * NG - 2, NG - 2)
            pool.wait_ge(wo_loaded, 32)
            pool.wait_ge(x_in[0], 16)
            for i in range(NT // 4):
                add_bo(i)
            sum_chunks(B * NG - 1, NG - 1)
            pool.wait_ge(x_in[1], 16)
            for i in range(NT // 4, NT // 2):
                add_bo(i)
            pool.wait_ge(ln_loaded, 32)
            with pool.Fori(0, NT) as n:
                add_ln_b(n)


def kernel(x, ctx_4096, mask_BxS2_ik0, L0_xattn_Wq, L0_xattn_bq, L0_xattn_Wk, L0_xattn_bk,
           L0_xattn_Wv, L0_xattn_bv, L0_xattn_Wo, L0_xattn_bo, L0_xattn_ln_g, L0_xattn_ln_b):
    import numpy as np
    import concourse.bacc as bacc
    from concourse.bass_utils import run_bass_kernel_spmd

    def c(a):
        return np.ascontiguousarray(a)

    def weight(w):
        return c(np.asarray(w).T.reshape(KT, P, D).transpose(1, 0, 2).reshape(P, KT * D))

    def column(v):
        return c(np.asarray(v).reshape(KT, P).T)

    x = np.asarray(x)
    context = np.asarray(ctx_4096)
    rows = np.arange(P)
    head_mask = ((rows[:, None] % 64) // HD == np.arange(4)[None, :]).astype(np.float32)
    arrays = {
        "ctxT": c(context.reshape(B, NP, SP_, KT, P).transpose(0, 1, 4, 3, 2)),
        "maskT": c(np.asarray(mask_BxS2_ik0).reshape(B, NC_, SC).transpose(0, 2, 1)),
        "xT": c(x.reshape(NQB, BPB * L, KT, P).transpose(0, 3, 2, 1)),
        "x_rows": c(x.reshape(ROWS, D)),
        "wqT": weight(L0_xattn_Wq), "wkT": weight(L0_xattn_Wk), "wvT": weight(L0_xattn_Wv),
        "woT": weight(L0_xattn_Wo),
        "bq": column(L0_xattn_bq), "bk": column(L0_xattn_bk), "bv": column(L0_xattn_bv),
        "bo": c(L0_xattn_bo), "ln_g": c(L0_xattn_ln_g), "ln_b": c(L0_xattn_ln_b),
        "ident": np.eye(P, dtype=np.float32), "head_mask": head_mask,
    }
    nc = bacc.Bacc("TRN2", target_bir_lowering=False, num_devices=1)
    ap = {n: nc.dram_tensor(n, a.shape, mybir.dt.from_np(a.dtype), kind="ExternalInput").ap()
          for n, a in arrays.items()}
    q_scratch = nc.dram_tensor("q_scratch", (B, 64, NG, 2, L), F32, kind="Internal").ap()
    att_scratch = nc.dram_tensor("att_scratch", (NG, 4, 2, HD, B, L), F32, kind="Internal").ap()
    out = nc.dram_tensor("out", (ROWS, D), F32, kind="ExternalOutput").ap()
    build_program(nc, ap["ctxT"], ap["maskT"], ap["xT"], ap["x_rows"], ap["wqT"], ap["wkT"],
                  ap["wvT"], ap["woT"], ap["bq"], ap["bk"], ap["bv"], ap["bo"], ap["ln_g"],
                  ap["ln_b"], ap["ident"], ap["head_mask"], q_scratch, att_scratch, out)
    r = run_bass_kernel_spmd(nc, [arrays], core_ids=[0])
    return r.results[0]["out"].reshape(B, L, D)
```
